# Optimizing a Trainium2 kernel written in Bass

```python
import numpy as np
import jax
import jax.numpy as jnp

def _softmax(x, axis=-1):
    return jax.nn.softmax(x, axis=axis)

def _gelu(x):
    return jax.nn.gelu(x, approximate=True)

def _silu(x):
    return jax.nn.silu(x)

def _sigmoid(x):
    return jax.nn.sigmoid(x)

def _layernorm(x, axis=-1, eps=1e-05):
    m = jnp.mean(x, axis=axis, keepdims=True)
    v = jnp.var(x, axis=axis, keepdims=True)
    return (x - m) / jnp.sqrt(v + eps)

def _scatter_add(tgt, idx, src, axis=0):
    return tgt.at[idx].add(src)

def _segment_sum(src, seg, n):
    return jax.ops.segment_sum(src, seg, n)
kernel_name = 'mk_flamingo_gated_d1_seqx_r4_076500'

def setup_inputs(seed: int=0):
    np.random.seed(seed)
    _w = jnp.asarray

    def _rec_inputs():
        import jax
        import jax.numpy as jnp
        _rk = jax.random.key(seed)
        x = -7.109e-05 + 0.9999 * jax.random.normal(jax.random.fold_in(_rk, 1), (4, 512, 1024), jnp.float32)
        _lenS = 512 - jax.random.randint(jax.random.fold_in(_rk, 7), (4,), 0, max(1, 512 // 4) + 1, jnp.int32)
        _lenS2 = 64 - jax.random.randint(jax.random.fold_in(_rk, 8), (4,), 0, max(1, 64 // 4) + 1, jnp.int32)
        _ctx_4096P = jax.random.normal(jax.random.fold_in(_rk, 11), (4, 16, 1024), jnp.float32)
        _ctx_4096c = jax.random.dirichlet(jax.random.fold_in(_rk, 511), 0.3 * jnp.ones((16,), jnp.float32), (4, 64))
        _ctx_4096t = jnp.einsum('bsk,bkd->bsd', _ctx_4096c, _ctx_4096P)
        _ctx_4096t = _ctx_4096t * jax.lax.rsqrt(jnp.mean(jnp.square(_ctx_4096t)) + 1e-12) * 0.953939
        ctx_4096 = -2.6191e-05 + 0.999952 * (_ctx_4096t + 0.3 * jax.random.normal(jax.random.fold_in(_rk, 611), (4, 64, 1024), jnp.float32))
        _g = jax.random.normal(jax.random.fold_in(_rk, 9001), (2, 1), jnp.float32)
        _g = jnp.sign(_g) * jnp.maximum(jnp.abs(_g), 1.0) + (_g == 0) * 1.0
        g_xattn = _g[0]
        g_ffn = _g[1]
        return (x, ctx_4096, g_xattn, g_ffn)
    x, ctx_4096, g_xattn, g_ffn = _rec_inputs()

    def _L0_xattn_setup():
        import jax, jax.numpy as jnp
        import numpy as np
        TEXT_DIM = 1024
        FEATURE_DIM = 1024

        def _xavier_uniform(key, shape):
            fan_in, fan_out = (shape[1], shape[0])
            limit = float(np.sqrt(6.0 / (fan_in + fan_out)))
            return jax.random.uniform(key, shape, jnp.float32, -limit, limit)
        key = jax.random.key(seed)
        k1, k2, k3, k4 = jax.random.split(key, 4)
        text = jax.random.normal(k1, (8, 512, TEXT_DIM), jnp.float32)
        features = jax.random.normal(k2, (8, 144, FEATURE_DIM), jnp.float32)
        Wq = _xavier_uniform(k3, (FEATURE_DIM, TEXT_DIM))
        bq = jnp.zeros((FEATURE_DIM,), jnp.float32)
        Wk = _xavier_uniform(k4, (FEATURE_DIM, FEATURE_DIM))
        bk = jnp.zeros((FEATURE_DIM,), jnp.float32)
        return {'text': text, 'features': features, 'Wq': Wq, 'bq': bq, 'Wk': Wk, 'bk': bk}
    _L0_xattn_all = _L0_xattn_setup()
    _L0_xattn_in = {k: v for k, v in _L0_xattn_all.items() if k in ('Wq', 'bq', 'Wk', 'bk')}
    del _L0_xattn_all

    def _L0_ffn_setup():
        import jax, jax.numpy as jnp
        import numpy as np

        @jax.custom_vjp
        def ste_sign(w):
            return jnp.sign(w)

        def _ste_fwd(w):
            return (jnp.sign(w), w)

        def _ste_bwd(w, g):
            mask = ((w > -1) & (w < 1)).astype(g.dtype)
            return (g * mask,)
        ste_sign.defvjp(_ste_fwd, _ste_bwd)
        key = jax.random.key(seed)
        k = jax.random.split(key, 6)
        B, S, H, O, E = (4, 512, 1024, 1024, 8)
        return {'x': jax.random.normal(k[0], (B, S, H), dtype=jnp.float32), 'weight': jax.random.normal(k[1], (O, H), dtype=jnp.float32) * 0.02, 'bias': jax.random.normal(k[2], (O,), dtype=jnp.float32) * 0.02, 'gate_w': jax.random.normal(k[3], (E, H), dtype=jnp.float32) * 0.02, 'in_channel_scale': jax.random.normal(k[4], (E, H), dtype=jnp.float32), 'out_channel_scale': jax.random.normal(k[5], (E, O), dtype=jnp.float32)}
    _L0_ffn_all = _L0_ffn_setup()
    _L0_ffn_in = {k: v for k, v in _L0_ffn_all.items() if k in ('weight', 'bias', 'gate_w', 'in_channel_scale', 'out_channel_scale')}
    del _L0_ffn_all
    return {'x': x, 'ctx_4096': ctx_4096, 'g_xattn': g_xattn, 'g_ffn': g_ffn, 'L0_xattn_Wq': _L0_xattn_in['Wq'], 'L0_xattn_bq': _L0_xattn_in['bq'], 'L0_xattn_Wk': _L0_xattn_in['Wk'], 'L0_xattn_bk': _L0_xattn_in['bk'], 'L0_ffn_weight': _L0_ffn_in['weight'], 'L0_ffn_bias': _L0_ffn_in['bias'], 'L0_ffn_gate_w': _L0_ffn_in['gate_w'], 'L0_ffn_in_channel_scale': _L0_ffn_in['in_channel_scale'], 'L0_ffn_out_channel_scale': _L0_ffn_in['out_channel_scale']}

def reference(x, ctx_4096, g_xattn, g_ffn, L0_xattn_Wq, L0_xattn_bq, L0_xattn_Wk, L0_xattn_bk, L0_ffn_weight, L0_ffn_bias, L0_ffn_gate_w, L0_ffn_in_channel_scale, L0_ffn_out_channel_scale):
    import jax
    import jax.numpy as jnp

    def _L0_xattn_ref(text, features, Wq, bq, Wk, bk):
        import jax, jax.numpy as jnp
        import numpy as np
        TEXT_DIM = 1024
        FEATURE_DIM = 1024

        def _xavier_uniform(key, shape):
            fan_in, fan_out = (shape[1], shape[0])
            limit = float(np.sqrt(6.0 / (fan_in + fan_out)))
            return jax.random.uniform(key, shape, jnp.float32, -limit, limit)
        Q = jnp.einsum('btx,dx->btd', text, Wq) + bq
        K = jnp.einsum('bpx,dx->bpd', features, Wk) + bk
        scale = 1.0 / jnp.sqrt(jnp.asarray(K.shape[-1], K.dtype))
        scores = jnp.einsum('btd,bpd->btp', Q, K) * scale
        attn = jax.nn.softmax(scores, axis=-1)
        attended = jnp.einsum('btp,bpd->btd', attn, features)
        return attended

    def _L0_ffn_ref(x, weight, bias, gate_w, in_channel_scale, out_channel_scale):
        import jax, jax.numpy as jnp
        import numpy as np

        @jax.custom_vjp
        def ste_sign(w):
            return jnp.sign(w)

        def _ste_fwd(w):
            return (jnp.sign(w), w)

        def _ste_bwd(w, g):
            mask = ((w > -1) & (w < 1)).astype(g.dtype)
            return (g * mask,)
        ste_sign.defvjp(_ste_fwd, _ste_bwd)
        B, S, H = x.shape
        xf = x.reshape(-1, H)
        router_logits = xf @ gate_w.T
        routing = jax.nn.softmax(router_logits.astype(jnp.float32), axis=1).astype(x.dtype)
        in_scale = routing @ in_channel_scale
        out_scale = routing @ out_channel_scale
        wb = ste_sign(weight)
        out = xf * in_scale @ wb.T * out_scale + bias
        return out.reshape(B, S, -1)
    x = x + jnp.tanh(g_xattn[0]) * _L0_xattn_ref(_layernorm(x, axis=-1), ctx_4096, L0_xattn_Wq, L0_xattn_bq, L0_xattn_Wk, L0_xattn_bk)
    x = x + jnp.tanh(g_ffn[0]) * _L0_ffn_ref(_layernorm(x, axis=-1), L0_ffn_weight, L0_ffn_bias, L0_ffn_gate_w, L0_ffn_in_channel_scale, L0_ffn_out_channel_scale)
    return x

_drawn_inputs = setup_inputs


def setup_inputs(seed=0):
    import zlib

    import numpy as np

    out = dict(_drawn_inputs(seed))
    spreads = {'L0_xattn_bq': (0.0, 0.353), 'L0_xattn_bk': (0.0, 0.8)}
    factors = {'L0_ffn_bias': 8.0}
    for name, (base, spread) in spreads.items():
        noise = np.random.default_rng([zlib.crc32(name.encode()), seed]).standard_normal(out[name].shape)
        drawn = base * np.exp(spread * noise) if base else spread * noise
        out[name] = jnp.asarray(drawn.astype(out[name].dtype))
    for name, factor in factors.items():
        out[name] = (out[name] * factor).astype(out[name].dtype)
    return out
```

```python
import concourse.bass as bass
from concourse import mybir
from contextlib import ExitStack


class Steps:

    def __init__(self, eng, sem):
        self.eng, self.sem, self.count, self.loop = eng, sem, 0, 0

    def done(self, instruction):
        instruction.then_inc(self.sem, 1)
        self.count += 1

    def wait(self):
        self.eng.wait_ge(self.sem, self.loop + self.count)


def gated_cross_attention_and_routed_ffn(nc, x_rows, x_cols, ctx_rows, ctx_cols, g_xattn, g_ffn, wq_rows, bq_cols,
                                         wk_cols, bk_cols, w_cols, ffn_bias, gate_w, in_scale, out_scale, y_rows):
    f32, f32r = mybir.dt.float32, mybir.dt.float32r
    ALU, ACT, AX = mybir.AluOpType, mybir.ActivationFunctionType, mybir.AxisListType

    P = 128
    T, D = x_rows.shape
    NB, NC = ctx_rows.shape[0], ctx_rows.shape[1]
    E = gate_w.shape[0]
    CH = D // P
    NT = T // P
    TPB = NT // NB
    H = D // 2
    CW = D + E
    AW = CW // 3
    KW = P
    EPS = 1e-5
    SC = float(D) ** -0.5
    CTX = NB * NC
    GRP = 32

    ctx = ExitStack()
    with ctx:
        def sb(name, shape, dt=f32):
            return ctx.enter_context(nc.sbuf_tensor(name, shape, dt))

        def sem(name):
            return ctx.enter_context(nc.semaphore(name))

        wk_sb = sb("wk_sb", [P, CH * D])
        wq_sb = sb("wq_sb", [P, CH * D])
        ctxT = sb("ctxT", [P, CH, CTX])
        kT = sb("kT", [P, CH, CTX])
        kqg = sb("kqg", [P, NB * CH * KW])
        signT = sb("signT", [P, CH, D], f32r)
        w_stage = sb("w_stage", [P, 2, D])
        ctxs = sb("ctxs", [P, NB * CW], f32r)
        scales = sb("scales", [P, 2, D], f32r)
        x_sb = sb("x_sb", [P, 2, D])
        xT_sb = sb("xT_sb", [P, 2, CH, P])
        x1 = sb("x1", [P, 2, D])
        aT_hi = sb("aT_hi", [P, 2, CH, P], f32r)
        aT_lo = sb("aT_lo", [P, 2, CH, P], f32r)
        ident = sb("ident", [P, P])
        ones = sb("ones", [P, P])
        cbias = sb("cbias", [P, CTX])
        cacc = sb("cacc", [P, CTX])
        gwT = sb("gwT", [P, CH, E])
        bqT = sb("bqT", [P, CH])
        bkT = sb("bkT", [P, CH])
        gates = sb("gates", [P, 2])
        tgates = sb("tgates", [P, 2])
        att_hi = sb("att_hi", [P, P], f32r)
        att_lo = sb("att_lo", [P, P], f32r)
        s_sb = sb("s_sb", [P, NC])
        e_sb = sb("e_sb", [P, NC])
        e2 = sb("e2", [P, 2, NC])
        route = sb("route", [P, 4, GRP])
        routeT = sb("routeT", [P, P], f32r)
        xgate = sb("xgate", [P, 2, E])
        logit = sb("logit", [P, E])
        eroute = sb("eroute", [P, E])
        hold = sb("hold", [P, 1])
        neg_half = sb("neg_half", [P, 1])
        st = sb("st", [P, 2, 6])
        mv0 = sb("mv0", [P, 2])
        mv1 = sb("mv1", [P, 2, 2])
        veps0 = sb("veps0", [P, 1])
        veps1 = sb("veps1", [P, 1])
        rstd0 = sb("rstd0", [P, 1])
        rstd1 = sb("rstd1", [P, 2])
        rfin = sb("rfin", [P, 2])
        nmax = sb("nmax", [P, 1])
        esum = sb("esum", [P, 1])
        erec = sb("erec", [P, 1])
        rmax = sb("rmax", [P, 1])
        rbias = sb("rbias", [P, 1])
        rsum = sb("rsum", [P, 1])
        rrec = sb("rrec", [P, 1])
        bank = [ctx.enter_context(nc.psum_tensor(f"bank{i}", [P, H], f32)) for i in range(8)]

        wk3 = wk_sb[:, :].rearrange("p (c d) -> p c d", c=CH)
        wq3 = wq_sb[:, :].rearrange("p (c d) -> p c d", c=CH)
        ctx_raw = wk_sb[:, 0:NB * CW].rearrange("p (b d) -> p b d", b=NB)
        scale_raw = wk_sb[:, NB * CW:NB * CW + 2 * D].rearrange("p (s d) -> p s d", s=2)
        bias_bc = wk_sb[:, NB * CW + 2 * D:NB * CW + 3 * D]
        os_sb = wq_sb[:, 0:2 * D].rearrange("p (s d) -> p s d", s=2)
        x1b = wq_sb[:, 2 * D:4 * D].rearrange("p (s d) -> p s d", s=2)
        y_sb = wq_sb[:, 4 * D:6 * D].rearrange("p (s d) -> p s d", s=2)
        a_sb = wq_sb[:, 6 * D:7 * D]
        gw = w_stage[0:E, 0, :]
        kqg4 = kqg[:, :].rearrange("p (b c w) -> p b c w", b=NB, c=CH)
        ctxs3 = ctxs[:, :].rearrange("p (b d) -> p b d", b=NB)

        small_loaded = sem("small_loaded")
        ctxT_loaded = sem("ctxT_loaded")
        wk_loaded = [sem(f"wk_loaded{c}") for c in range(CH)]
        wq_loaded = [sem(f"wq_loaded{c}") for c in range(CH)]
        ctx_loaded = sem("ctx_loaded")
        scale_loaded = sem("scale_loaded")
        bias_loaded = sem("bias_loaded")
        w_loaded = [sem(f"w_loaded{s}") for s in range(2)]
        x_loaded = [sem(f"x_loaded{s}") for s in range(2)]
        xT_loaded = [sem(f"xT_loaded{s}") for s in range(2)]
        y_stored = [sem(f"y_stored{s}") for s in range(2)]
        consts = sem("consts")
        scale_zero = sem("scale_zero")
        gw_ready = sem("gw_ready")
        gwT_made = sem("gwT_made")
        gwT_ready = sem("gwT_ready")
        tanh_ready = sem("tanh_ready")
        k_made = sem("k_made")
        kT_act = sem("kT_act")
        kT_dve = sem("kT_dve")
        wq_centred = sem("wq_centred")
        kq_made = sem("kq_made")
        kq_act = sem("kq_act")
        kq_dve = sem("kq_dve")
        cacc_ready = sem("cacc_ready")
        cbias_made = sem("cbias_made")
        cbias_ready = sem("cbias_ready")
        cg_made = sem("cg_made")
        cg_ready = sem("cg_ready")
        ctx_hi = sem("ctx_hi")
        ctx_lo = sem("ctx_lo")
        cg_hi = sem("cg_hi")
        cg_lo = sem("cg_lo")
        scale_hi = sem("scale_hi")
        scale_lo = sem("scale_lo")
        sign_ready = sem("sign_ready")
        gb_ready = sem("gb_ready")
        act_steps = sem("act_steps")
        dve_steps = sem("dve_steps")
        pool_steps = sem("pool_steps")
        scores_made = sem("scores_made")
        veps0_ready = sem("veps0_ready")
        rstd0_ready = sem("rstd0_ready")
        nmax_ready = sem("nmax_ready")
        exp_ready = sem("exp_ready")
        e2_ready = sem("e2_ready")
        attT_made = sem("attT_made")
        att_hi_ready = sem("att_hi_ready")
        att_lo_ready = sem("att_lo_ready")
        attended_made = sem("attended_made")
        x1_ready = sem("x1_ready")
        x1b_ready = sem("x1b_ready")
        veps1_ready = sem("veps1_ready")
        rstd1_ready = sem("rstd1_ready")
        rbias_ready = sem("rbias_ready")
        rexp_ready = sem("rexp_ready")
        route_ready = sem("route_ready")
        routeT_made = sem("routeT_made")
        route_hi = sem("route_hi")
        route_lo = sem("route_lo")
        is_made = sem("is_made")
        os_made = sem("os_made")
        os_ready = sem("os_ready")
        a_ready = sem("a_ready")
        aT_made = sem("aT_made")
        aT_hi_ready = sem("aT_hi_ready")
        aT_lo_ready = sem("aT_lo_ready")
        ffn_made = sem("ffn_made")
        scaled_ready = sem("scaled_ready")
        y_ready = sem("y_ready")

        block = ctx.enter_context(nc.Block())

        def half(h):
            return slice(h * H, (h + 1) * H)

        def pairs(eng, steps, per_pair, iteration):
            with eng.Fori(0, (NT - 4) // 2) as i:
                if steps is not None:
                    start, steps.loop = steps.count, i * per_pair
                for c in range(2):
                    iteration(2 * i + (3 + c), (3 + c) % 2, (i + 2) // (TPB // 2))
                if steps is not None:
                    assert steps.count - start == per_pair, steps.count - start
                    steps.loop, steps.count = 0, start + per_pair * ((NT - 4) // 2)

        @block.sync
        def _(sp):
            sp.dma_start(gw[:, :], gate_w).then_inc(small_loaded, 16)
            sp.dma_start(ctxT[:, :, :], ctx_cols).then_inc(ctxT_loaded, 16)
            for c in range(CH):
                sp.dma_start(wk3[:, c, :], wk_cols[c * P:(c + 1) * P, :]).then_inc(wk_loaded[c], 16)
            for c in range(CH):
                sp.dma_start(wq3[:, c, :], wq_rows[c * P:(c + 1) * P, :]).then_inc(wq_loaded[c], 16)

            def load(t, s):
                sp.dma_start(xT_sb[:, s, :, :], x_cols[bass.ds(t * P, P), :, :]).then_inc(xT_loaded[s], 16)
                sp.dma_start(x_sb[:, s, :], x_rows[bass.ds(t * P, P), :]).then_inc(x_loaded[s], 16)

            for t in range(2):
                load(t, t)
            sp.wait_ge(k_made, CH)
            for d in range(2):
                sp.dma_start(ctx_raw[d * NC:(d + 1) * NC, :, 0:D], ctx_rows.rearrange("b p d -> p b d"))\
                  .then_inc(ctx_loaded, 16)
            sp.dma_start(bias_bc, ffn_bias.rearrange("(a n) -> a n", a=1).to_broadcast([P, D])).then_inc(bias_loaded, 16)
            sp.wait_ge(scale_zero, 1)
            for g in range(4):
                for n, src in enumerate((in_scale, out_scale)):
                    sp.dma_start(scale_raw[g * GRP:g * GRP + E, n, :], src).then_inc(scale_loaded, 16)
            for c in range(CH):
                if c >= 2:
                    sp.wait_ge(sign_ready, c - 1)
                sp.dma_start(w_stage[:, c % 2, :], w_cols[c * P:(c + 1) * P, :]).then_inc(w_loaded[c % 2], 16)

            def load_into_used(t, s):
                sp.wait_ge(scores_made, t - 1)
                sp.wait_ge(x1_ready, t - 1)
                load(t, s)

            def store(t, s):
                sp.wait_ge(y_ready, 2 * t + 2)
                sp.dma_start(y_rows[bass.ds(t * P, P), :], y_sb[:, s, :]).then_inc(y_stored[s], 16)

            for t in (2, 3):
                load_into_used(t, t % 2)
            with sp.Fori(0, (NT - 4) // 2) as i:
                for c in range(2):
                    store(2 * i + c, c)
                    load_into_used(2 * i + (4 + c), c)
            for t in range(NT - 4, NT):
                store(t, t % 2)
            for s in range(2):
                sp.wait_ge(y_stored[s], 16 * (NT // 2))

        @block.gpsimd
        def _(pool):
            steps = Steps(pool, pool_steps)
            steps.done(nc.gpsimd.memset(ident[:, :], 0.0))
            nc.gpsimd.memset(ones[:, :], 1.0)
            nc.gpsimd.memset(neg_half[:, :], -0.5)
            nc.gpsimd.memset(route[:, :, :], 0.0)
            nc.gpsimd.memset(kqg4[:, :, :, NC + E:KW], 0.0)
            steps.wait()
            nc.gpsimd.affine_select(out=ident[:, :], in_=ident[:, :], compare_op=ALU.not_equal, fill=1.0, base=0,
                                    pattern=[[-1, P]], channel_multiplier=1).then_inc(consts, 1)
            pool.wait_ge(k_made, CH)
            nc.gpsimd.memset(scale_raw, 0.0).then_inc(scale_zero, 1)

            def iteration(j, s, b=None, prev=True, cur=True, nxt=True):
                def add_up(h):
                    if h == 0:
                        pool.wait_ge(x1b_ready, j)
                    pool.wait_ge(scaled_ready, 2 * j + (h - 1))
                    nc.gpsimd.tensor_tensor(y_sb[:, 1 - s, half(h)], y_sb[:, 1 - s, half(h)],
                                            x1b[:, 1 - s, half(h)], ALU.add).then_inc(y_ready, 1)

                if nxt:
                    pool.wait_ge(veps0_ready, j + 2)
                    nc.gpsimd.tensor_tensor(rstd0[:, :], veps0[:, :], neg_half[:, :], ALU.pow).then_inc(rstd0_ready, 1)
                if prev:
                    add_up(0)
                if prev:
                    add_up(1)
                if nxt:
                    pool.wait_ge(veps1_ready, j + 2)
                    nc.gpsimd.tensor_tensor(rstd1[:, 1 - s:2 - s], veps1[:, :], neg_half[:, :], ALU.pow)\
                      .then_inc(rstd1_ready, 1)
                    if prev:
                        pool.wait_ge(y_ready, 2 * j)
                    nc.gpsimd.tensor_tensor(x1b[:, 1 - s, :], x1[:, 1 - s, :], bias_bc, ALU.add).then_inc(x1b_ready, 1)

            pool.wait_ge(gb_ready, 1)
            iteration(-1, 1, prev=False, cur=False)
            iteration(0, 0, prev=False)
            iteration(1, 1)
            iteration(2, 0)
            pairs(pool, None, 0, iteration)
            iteration(NT - 1, 1, nxt=False)
            iteration(NT, 0, cur=False, nxt=False)

        @block.scalar
        def _(act):
            act.dma_start(bqT[:, :], bq_cols).then_inc(small_loaded, 16)
            act.dma_start(bkT[:, :], bk_cols).then_inc(small_loaded, 16)
            act.dma_start(gates[:, 0:1], g_xattn.rearrange("(a n) -> a n", a=1).to_broadcast([P, 1])).then_inc(small_loaded, 16)
            act.dma_start(gates[:, 1:2], g_ffn.rearrange("(a n) -> a n", a=1).to_broadcast([P, 1])).then_inc(small_loaded, 16)
            act.wait_ge(small_loaded, 80)
            nc.scalar.activation(tgates[:, :], gates[:, :], ACT.Tanh).then_inc(tanh_ready, 1)
            for c in range(0, CH, 2):
                act.wait_ge(k_made, c + 1)
                nc.scalar.activation(kT[:, c, :], bank[c][:, 0:CTX], ACT.Identity, bias=bkT[:, c:c + 1]).then_inc(kT_act, 1)
            act.wait_ge(ctx_loaded, 32)
            for b in range(NB):
                nc.scalar.activation(ctxs3[:, b, 0:D], ctx_raw[:, b, 0:D], ACT.Copy).then_inc(ctx_hi, 1)
            act.wait_ge(scale_loaded, 16 * 8)
            nc.scalar.activation(scales[:, :, :], scale_raw, ACT.Copy).then_inc(scale_hi, 1)
            for c in range(0, CH, 2):
                act.wait_ge(kq_made, c + 1)
                nc.scalar.activation(kqg4[:, :, c, 0:NC], bank[c][:, 0:CTX].rearrange("p (b n) -> p b n", b=NB),
                                     ACT.Copy).then_inc(kq_act, 1)
                for n in range(c, c + 2):
                    act.wait_ge(w_loaded[n % 2], 16 * (n // 2 + 1))
                    nc.scalar.activation(signT[:, n, :], w_stage[:, n % 2, :], ACT.Sign).then_inc(sign_ready, 1)
            act.wait_ge(cbias_made, 1)
            nc.scalar.activation(cbias[:, :], bank[0][:, 0:CTX], ACT.Copy, scale=SC).then_inc(cbias_ready, 1)
            act.wait_ge(cg_ready, 1)
            nc.scalar.activation(ctxs3[:, :, D:CW], ctx_raw[:, :, D:CW], ACT.Copy).then_inc(cg_hi, 1)

            def iteration(j, s, b=None, prev=True, cur=True, nxt=True):
                if nxt:
                    act.wait_ge(nmax_ready, j + 2)
                    nc.scalar.activation(e_sb[:, :], s_sb[:, :], ACT.Exp, bias=nmax[:, 0:1],
                                         accum_out=esum[:, 0:1]).then_inc(exp_ready, 1)
                if cur:
                    act.wait_ge(routeT_made, j + 1)
                    nc.scalar.activation(routeT[:, :], bank[2][:, 0:P], ACT.Copy).then_inc(route_hi, 1)
                    for h in range(2):
                        act.wait_ge(os_made, 2 * j + (h + 1))
                        nc.scalar.activation(os_sb[:, s, half(h)], bank[h][:, :], ACT.Copy).then_inc(os_ready, 1)
                    for h in range(2):
                        act.wait_ge(aT_made, 2 * j + (h + 1))
                        nc.scalar.activation(aT_hi[:, s, h * CH // 2:(h + 1) * CH // 2, :],
                                             bank[3 + h][:, :].rearrange("p (c t) -> p c t", t=P), ACT.Copy)\
                          .then_inc(aT_hi_ready, 1)
                if nxt:
                    act.wait_ge(attT_made, j + 2)
                    nc.scalar.activation(att_hi[:, :], bank[7][:, 0:P], ACT.Copy).then_inc(att_hi_ready, 1)
                    act.wait_ge(rbias_ready, j + 2)
                    nc.scalar.activation(eroute[:, :], logit[:, :], ACT.Exp, bias=rbias[:, 0:1],
                                         scale=rstd1[:, 1 - s:2 - s], accum_out=rsum[:, 0:1]).then_inc(rexp_ready, 1)

            iteration(-1, 1, prev=False, cur=False)
            iteration(0, 0, prev=False)
            iteration(1, 1)
            iteration(2, 0)
            pairs(act, None, 0, iteration)
            iteration(NT - 1, 1, nxt=False)

        @block.vector
        def _(dve):
            steps = Steps(dve, dve_steps)

            def mean_var(src, out):
                for h in range(2):
                    last = nc.vector.bn_stats(st[0:src.shape[0], h, :], src[:, half(h)])
                steps.done(last)
                steps.wait()
                nc.vector.memset(hold[:, :], 0.0)
                steps.done(nc.vector.bn_aggr(out, st[0:src.shape[0], :, :]))
                steps.wait()

            dve.wait_ge(small_loaded, 80)
            mean_var(gw[:, :], mv0[0:E, :])
            nc.vector.tensor_scalar(gw[:, :], gw[:, :], mv0[0:E, 0:1], None, ALU.subtract).then_inc(gw_ready, 1)
            dve.wait_ge(gwT_made, 1)
            steps.done(nc.vector.tensor_copy(gwT[:, :, :], bank[7][:, 0:CH * E].rearrange("p (c e) -> p c e", e=E)))
            steps.wait()
            for b in range(NB):
                last = nc.vector.tensor_copy(kqg4[:, b, :, NC:NC + E], gwT[:, :, :])
            last.then_inc(gwT_ready, 1)
            for c in range(CH):
                dve.wait_ge(wq_loaded[c], 16)
                mean_var(wq3[:, c, :], mv0[:, :])
                nc.vector.tensor_scalar(wq3[:, c, :], wq3[:, c, :], mv0[:, 0:1], None, ALU.subtract).then_inc(wq_centred, 1)
            for c in range(1, CH, 2):
                dve.wait_ge(k_made, c + 1)
                nc.vector.tensor_scalar(kT[:, c, :], bank[c][:, 0:CTX], bkT[:, c:c + 1], None, ALU.add).then_inc(kT_dve, 1)
            dve.wait_ge(kT_dve, CH // 2)
            dve.wait_ge(kT_act, CH // 2)
            for c in range(CH):
                if c == 0:
                    ins = nc.vector.tensor_scalar(cacc[:, :], kT[:, c, :], bqT[:, c:c + 1], None, ALU.mult)
                else:
                    ins = nc.vector.scalar_tensor_tensor(out=cacc[:, :], in0=kT[:, c, :], scalar=bqT[:, c:c + 1],
                                                         in1=cacc[:, :], op0=ALU.mult, op1=ALU.add)
                if c == CH - 1:
                    ins.then_inc(cacc_ready, 1)
                else:
                    steps.done(ins)
                    steps.wait()
            for b in range(NB):
                dve.wait_ge(ctx_hi, b + 1)
                nc.vector.tensor_tensor(ctxs3[NC:P, b, 0:D], ctx_raw[NC:P, b, 0:D], ctxs3[NC:P, b, 0:D].bitcast(f32),
                                        ALU.subtract).then_inc(ctx_lo, 1)
            dve.wait_ge(scale_hi, 1)
            for g in (1, 3):
                rows = slice(g * GRP, (g + 1) * GRP)
                nc.vector.tensor_tensor(scales[rows, :, :], scale_raw[rows, :, :], scales[rows, :, :].bitcast(f32),
                                        ALU.subtract).then_inc(scale_lo, 1)
            dve.wait_ge(bias_loaded, 16)
            dve.wait_ge(tanh_ready, 1)
            nc.vector.tensor_scalar(bias_bc, bias_bc, tgates[:, 1:2], None, ALU.mult).then_inc(gb_ready, 1)
            for c in range(1, CH, 2):
                dve.wait_ge(kq_made, c + 1)
                nc.vector.tensor_copy(kqg4[:, :, c, 0:NC], bank[c][:, 0:CTX].rearrange("p (b n) -> p b n", b=NB))\
                  .then_inc(kq_dve, 1)
            dve.wait_ge(cg_made, 1)
            for b in range(NB):
                rows = slice((b % 2) * NC, (b % 2 + 1) * NC)
                for d in range(2):
                    last = nc.vector.tensor_copy(ctx_raw[d * NC:(d + 1) * NC, b, D:CW], bank[1 + b // 2][rows, NC:NC + E])
            last.then_inc(cg_ready, 1)
            dve.wait_ge(cg_hi, 1)
            nc.vector.tensor_tensor(ctxs3[NC:P, :, D:CW], ctx_raw[NC:P, :, D:CW], ctxs3[NC:P, :, D:CW].bitcast(f32),
                                    ALU.subtract).then_inc(cg_lo, 1)

            def iteration(j, s, b=None, prev=True, cur=True, nxt=True):
                n = 1 - s

                def scale_output(h):
                    dve.wait_ge(ffn_made, 2 * j + (h - 1))
                    nc.vector.scalar_tensor_tensor(out=y_sb[:, n, half(h)], in0=bank[5 + h][:, :],
                                                   scalar=rfin[:, n:n + 1], in1=os_sb[:, n, half(h)],
                                                   op0=ALU.mult, op1=ALU.mult).then_inc(scaled_ready, 1)

                def low_half(h):
                    dve.wait_ge(aT_hi_ready, 2 * j + (h + 1))
                    chunks = slice(h * CH // 2, (h + 1) * CH // 2)
                    nc.vector.tensor_tensor(aT_lo[:, s, chunks, :], bank[3 + h][:, :].rearrange("p (c t) -> p c t", t=P),
                                            aT_hi[:, s, chunks, :].bitcast(f32), ALU.subtract).then_inc(aT_lo_ready, 1)

                if nxt:
                    dve.wait_ge(x_loaded[n], 16 * ((j + 1) // 2) + 16)
                    mean_var(x_sb[:, n, :], mv0[:, :])
                    nc.vector.tensor_scalar(veps0[:, :], mv0[:, 1:2], EPS, float(D), ALU.add, ALU.mult).then_inc(veps0_ready, 1)
                if prev:
                    if not (isinstance(j, int) and j < 3):
                        dve.wait_ge(y_stored[n], stored(j))
                    scale_output(0)
                if nxt:
                    dve.wait_ge(scores_made, j + 2)
                    dve.wait_ge(rstd0_ready, j + 2)
                    steps.done(nc.vector.scalar_tensor_tensor(
                        out=s_sb[:, :], in0=bank[7][:, 0:NC], scalar=rstd0[:, 0:1],
                        in1=cbias[:, bass.ds(b * NC, NC)], op0=ALU.mult, op1=ALU.add))
                    nc.vector.tensor_copy(xgate[:, n, :], bank[7][:, NC:NC + E])
                    steps.wait()
                    nc.vector.reduce_max(nmax[:, :], s_sb[:, :], AX.X, negate=True).then_inc(nmax_ready, 1)
                if cur:
                    dve.wait_ge(route_hi, j + 1)
                    nc.vector.tensor_tensor(routeT[NC:P, :], bank[2][NC:P, 0:P], routeT[NC:P, :].bitcast(f32),
                                            ALU.subtract).then_inc(route_lo, 1)
                    for h in range(2):
                        dve.wait_ge(is_made, 2 * j + (h + 1))
                        nc.vector.scalar_tensor_tensor(out=a_sb[:, half(h)], in0=x1[:, s, half(h)],
                                                       scalar=mv1[:, s, 0:1], in1=bank[3 + h][:, :],
                                                       op0=ALU.subtract, op1=ALU.mult).then_inc(a_ready, 1)
                if nxt:
                    dve.wait_ge(exp_ready, j + 2)
                    steps.done(nc.vector.reciprocal(erec[:, :], esum[:, :]))
                    steps.wait()
                    nc.vector.tensor_scalar(e2[:, :, :], e_sb[:, :].unsqueeze(1).to_broadcast([P, 2, NC]),
                                            erec[:, 0:1], tgates[:, 0:1], ALU.mult, ALU.mult).then_inc(e2_ready, 1)
                if cur:
                    low_half(0)
                if nxt:
                    dve.wait_ge(att_hi_ready, j + 2)
                    nc.vector.tensor_tensor(att_lo[:, :], bank[7][:, 0:P], att_hi[:, :].bitcast(f32),
                                            ALU.subtract).then_inc(att_lo_ready, 1)
                if cur:
                    low_half(1)
                if prev:
                    scale_output(1)
                if nxt:
                    dve.wait_ge(attended_made, j + 2)
                    if not (isinstance(j, int) and j < 1):
                        dve.wait_ge(x1b_ready, j)
                    for i in range(3):
                        cols = slice(i * AW, min((i + 1) * AW, D))
                        last = nc.vector.tensor_tensor(x1[:, n, cols], x_sb[:, n, cols],
                                                       bank[i][:, 0:cols.stop - cols.start], ALU.add)
                    last.then_inc(x1_ready, 1)
                    steps.done(nc.vector.tensor_tensor(logit[:, :], xgate[:, n, :], bank[2][:, D - 2 * AW:AW], ALU.add))
                    steps.wait()
                    nc.vector.reduce_max(rmax[:, :], logit[:, :], AX.X, negate=True)
                    mean_var(x1[:, n, :], mv1[:, n, :])
                    nc.vector.tensor_scalar(veps1[:, :], mv1[:, n, 1:2], EPS, None, ALU.add).then_inc(veps1_ready, 1)
                    dve.wait_ge(rstd1_ready, j + 2)
                    nc.vector.tensor_scalar(rbias[:, :], rmax[:, :], rstd1[:, n:n + 1], None, ALU.mult)\
                      .then_inc(rbias_ready, 1)
                    nc.vector.tensor_scalar(rfin[:, n:n + 1], rstd1[:, n:n + 1], tgates[:, 1:2], None, ALU.mult)
                    dve.wait_ge(rexp_ready, j + 2)
                    steps.done(nc.vector.reciprocal(rrec[:, :], rsum[:, :]))
                    steps.wait()
                    nc.vector.tensor_scalar(route[:, :, 0:E], eroute[:, :].unsqueeze(1).to_broadcast([P, 4, E]),
                                            rrec[:, 0:1], None, ALU.mult).then_inc(route_ready, 1)

            def stored(j):
                return 16 * ((j - 1) // 2)

            dve.wait_ge(cbias_ready, 1)
            iteration(-1, 1, 0, prev=False, cur=False)
            iteration(0, 0, 0, prev=False)
            iteration(1, 1, 0)
            iteration(2, 0, 0)
            pairs(dve, steps, 2 * 8, iteration)
            iteration(NT - 1, 1, nxt=False)
            iteration(NT, 0, cur=False, nxt=False)

        @block.tensor
        def _(pe):
            pe.wait_ge(consts, 1)
            pe.wait_ge(gw_ready, 1)
            for c in range(CH):
                last = nc.tensor.transpose(bank[7][:, c * E:(c + 1) * E], gw[:, c * P:(c + 1) * P], ident[0:E, 0:E])
            last.then_inc(gwT_made, 1)
            pe.wait_ge(ctxT_loaded, 16)
            for c in range(CH):
                pe.wait_ge(wk_loaded[c], 16)
                for m in range(CH):
                    if c == 0 and m == 7:
                        pe.wait_ge(gwT_ready, 1)
                    last = nc.tensor.matmul(bank[m][:, 0:CTX], wk3[:, c, m * P:(m + 1) * P], ctxT[:, c, :],
                                            start=(c == 0), stop=(c == CH - 1))
                    if c == CH - 1:
                        last.then_inc(k_made, 1)
            pe.wait_ge(kT_act, CH // 2)
            pe.wait_ge(kT_dve, CH // 2)
            pe.wait_ge(wq_centred, CH)
            for m in range(CH):
                for c in range(CH):
                    last = nc.tensor.matmul(bank[m][:, 0:CTX], wq3[:, c, m * P:(m + 1) * P], kT[:, c, :],
                                            start=(c == 0), stop=(c == CH - 1))
                last.then_inc(kq_made, 1)
            pe.wait_ge(cacc_ready, 1)
            pe.wait_ge(kq_act, 1)
            nc.tensor.matmul(bank[0][:, 0:CTX], ones[:, :], cacc[:, :], start=True, stop=True).then_inc(cbias_made, 1)
            pe.wait_ge(kq_act, CH // 2)
            pe.wait_ge(kq_dve, CH // 2)
            for m in range(CTX // P):
                for c in range(CH):
                    last = nc.tensor.matmul(bank[1 + m][:, 0:KW], ctxT[:, c, m * P:(m + 1) * P], kqg4[:, 0, c, :],
                                            start=(c == 0), stop=(c == CH - 1))
            last.then_inc(cg_made, 1)

            def ffn(t, s, quarters):
                for q in quarters:
                    h, part = q // 4, q % 4 // 2
                    if q % 4 == 0 and not (isinstance(t, int) and t < 1):
                        pe.wait_ge(scaled_ready, 2 * t + (h - 1))
                    if q == 0:
                        pe.wait_ge(aT_hi_ready, 2 * t + 2)
                    if q == 2:
                        pe.wait_ge(aT_lo_ready, 2 * t + 2)
                    src = (aT_hi, aT_lo)[part]
                    for c in range(q % 2 * 4, q % 2 * 4 + 4):
                        last = nc.tensor.matmul(bank[5 + h][:, :], src[:, s, c, :], signT[:, c, half(h)],
                                                start=(part == 0 and c == 0), stop=(part == 1 and c == CH - 1))
                    if q % 4 == 3:
                        last.then_inc(ffn_made, 1)

            def iteration(j, s, b=None, prev=True, cur=True, nxt=True):
                n = 1 - s
                if prev:
                    ffn(j - 1, n, range(4))
                if nxt:
                    pe.wait_ge(xT_loaded[n], 16 * ((j + 1) // 2) + 16)
                    for c in range(CH):
                        last = nc.tensor.matmul(bank[7][:, 0:KW], xT_sb[:, n, c, :],
                                                kqg[:, bass.ds(b * (CH * KW) + c * KW, KW)],
                                                start=(c == 0), stop=(c == CH - 1))
                    last.then_inc(scores_made, 1)
                if cur:
                    pe.wait_ge(route_ready, j + 1)
                    nc.tensor.transpose(bank[2][:, 0:P], route[:, :, :].rearrange("p g e -> p (g e)"), ident[:, :])\
                      .then_inc(routeT_made, 1)
                if prev:
                    ffn(j - 1, n, range(4, 5))
                if cur:
                    pe.wait_ge(route_hi, j + 1)
                    pe.wait_ge(route_lo, j + 1)
                    for k, first, made in ((0, 3, is_made), (1, 0, os_made)):
                        for h in range(2):
                            nc.tensor.matmul(bank[first + h][:, :], routeT[:, :], scales[:, k, half(h)],
                                             start=True, stop=True).then_inc(made, 1)
                if prev:
                    ffn(j - 1, n, range(5, 7))
                if cur:
                    for h in range(2):
                        pe.wait_ge(a_ready, 2 * j + (h + 1))
                        for c in range(CH // 2):
                            k = h * CH // 2 + c
                            last = nc.tensor.transpose(bank[3 + h][:, c * P:(c + 1) * P], a_sb[:, k * P:(k + 1) * P],
                                                       ident[:, :])
                        last.then_inc(aT_made, 1)
                if nxt:
                    pe.wait_ge(e2_ready, j + 2)
                    nc.tensor.transpose(bank[7][:, 0:P], e2[:, :, :].rearrange("p a n -> p (a n)"), ident[:, :])\
                      .then_inc(attT_made, 1)
                if prev:
                    ffn(j - 1, n, range(7, 8))
                if nxt:
                    pe.wait_ge(att_hi_ready, j + 2)
                    pe.wait_ge(att_lo_ready, j + 2)
                    if not (isinstance(j, int) and j < 0):
                        pe.wait_ge(os_ready, 2 * j + 2)
                    for i in range(3):
                        for part, src in enumerate((att_hi, att_lo)):
                            last = nc.tensor.matmul(bank[i][:, 0:AW], src[:, :], ctxs[:, bass.ds(b * CW + i * AW, AW)],
                                                    start=(part == 0), stop=(part == 1))
                    last.then_inc(attended_made, 1)

            pe.wait_ge(cbias_ready, 1)
            pe.wait_ge(ctx_lo, NB)
            pe.wait_ge(cg_lo, 1)
            pe.wait_ge(scale_lo, 2)
            iteration(-1, 1, 0, prev=False, cur=False)
            iteration(0, 0, 0, prev=False)
            pe.wait_ge(sign_ready, CH)
            iteration(1, 1, 0)
            iteration(2, 0, 0)
            pairs(pe, None, 0, iteration)
            iteration(NT - 1, 1, nxt=False)
            iteration(NT, 0, cur=False, nxt=False)


def kernel(**inputs):
    import numpy as np
    import concourse.bacc as bacc
    from concourse.bass_utils import run_bass_kernel_spmd

    P = 128
    a = {k: np.asarray(v) for k, v in inputs.items()}
    x = a["x"].reshape(-1, a["x"].shape[-1])
    T, D = x.shape
    CH = D // P
    ctx = a["ctx_4096"]

    def columns(v):
        return v.reshape(CH, P, -1).transpose(1, 0, 2)

    arrays = {
        "x_rows": x,
        "x_cols": x.reshape(T // P, P, CH, P).transpose(0, 3, 2, 1).reshape(T, CH, P),
        "ctx_rows": ctx,
        "ctx_cols": columns(ctx.reshape(-1, D).T),
        "g_xattn": a["g_xattn"],
        "g_ffn": a["g_ffn"],
        "wq_rows": a["L0_xattn_Wq"],
        "bq_cols": columns(a["L0_xattn_bq"][:, None])[:, :, 0],
        "wk_cols": a["L0_xattn_Wk"].T,
        "bk_cols": columns(a["L0_xattn_bk"][:, None])[:, :, 0],
        "w_cols": a["L0_ffn_weight"].T,
        "ffn_bias": a["L0_ffn_bias"],
        "gate_w": a["L0_ffn_gate_w"],
        "in_scale": a["L0_ffn_in_channel_scale"],
        "out_scale": a["L0_ffn_out_channel_scale"],
    }
    nc = bacc.Bacc("TRN2", target_bir_lowering=False, num_devices=1)
    feeds, args = {}, []
    for name, v in arrays.items():
        v = np.ascontiguousarray(v)
        feeds[f"in_{name}"] = v
        args.append(nc.dram_tensor(f"in_{name}", v.shape, mybir.dt.from_np(v.dtype), kind="ExternalInput").ap())
    args.append(nc.dram_tensor("out_y", (T, D), mybir.dt.float32, kind="ExternalOutput").ap())
    gated_cross_attention_and_routed_ffn(nc, *args)
    r = run_bass_kernel_spmd(nc, [feeds], core_ids=[0])
    return r.results[0]["out_y"].reshape(a["x"].shape)
```

```python
import concourse.bass as bass
from concourse import mybir
from contextlib import ExitStack


class Steps:

    def __init__(self, eng, sem):
        self.eng, self.sem, self.count, self.loop = eng, sem, 0, 0

    def done(self, instruction):
        instruction.then_inc(self.sem, 1)
        self.count += 1

    def wait(self):
        self.eng.wait_ge(self.sem, self.loop + self.count)


def gated_cross_attention_and_routed_ffn(nc, x_rows, x_cols, ctx_rows, ctx_cols, g_xattn, g_ffn, wq_rows, bq_cols,
                                         wk_cols, bk_cols, w_cols, ffn_bias, gate_w, in_scale, out_scale, y_rows):
    f32, f32r = mybir.dt.float32, mybir.dt.float32r
    ALU, ACT, AX = mybir.AluOpType, mybir.ActivationFunctionType, mybir.AxisListType

    P = 128
    T, D = x_rows.shape
    NB, NC = ctx_rows.shape[0], ctx_rows.shape[1]
    E = gate_w.shape[0]
    CH = D // P
    NT = T // P
    TPB = NT // NB
    H = D // 2
    CW = D + E
    AW = CW // 3
    KW = P
    EPS = 1e-5
    SC = float(D) ** -0.5
    CTX = NB * NC
    GRP = 32

    ctx = ExitStack()
    with ctx:
        def sb(name, shape, dt=f32):
            return ctx.enter_context(nc.sbuf_tensor(name, shape, dt))

        def sem(name):
            return ctx.enter_context(nc.semaphore(name))

        wk_sb = sb("wk_sb", [P, CH * D])
        wq_sb = sb("wq_sb", [P, CH * D])
        ctxT = sb("ctxT", [P, CH, CTX])
        kT = sb("kT", [P, CH, CTX])
        kqg = sb("kqg", [P, NB * CH * KW])
        signT = sb("signT", [P, CH, D], f32r)
        w_stage = sb("w_stage", [P, 2, D])
        ctxs = sb("ctxs", [P, NB * CW], f32r)
        scales = sb("scales", [P, 2, D], f32r)
        x_sb = sb("x_sb", [P, 2, D])
        xT_sb = sb("xT_sb", [P, 2, CH, P])
        x1 = sb("x1", [P, 2, D])
        aT_hi = sb("aT_hi", [P, 2, CH, P], f32r)
        aT_lo = sb("aT_lo", [P, 2, CH, P], f32r)
        ident = sb("ident", [P, P])
        ones = sb("ones", [P, P])
        cbias = sb("cbias", [P, CTX])
        cacc = sb("cacc", [P, CTX])
        cgs = sb("cgs", [P, CTX // P, E])
        wq_mean = sb("wq_mean", [P, CH])
        nmean0 = sb("nmean0", [P, 1])
        ssq0 = sb("ssq0", [P, 1])
        eps_d = sb("eps_d", [P, 1])
        bqT = sb("bqT", [P, CH])
        bkT = sb("bkT", [P, CH])
        gates = sb("gates", [P, 2])
        tgates = sb("tgates", [P, 2])
        att_hi = sb("att_hi", [P, P], f32r)
        att_lo = sb("att_lo", [P, P], f32r)
        s_sb = sb("s_sb", [P, NC])
        e_sb = sb("e_sb", [P, NC])
        e2 = sb("e2", [P, 2, NC])
        route = sb("route", [P, 4, GRP])
        routeT = sb("routeT", [P, P], f32r)
        xgate = sb("xgate", [P, 2, E])
        logit = sb("logit", [P, E])
        eroute = sb("eroute", [P, E])
        hold = sb("hold", [P, 1])
        neg_half = sb("neg_half", [P, 1])
        st = sb("st", [P, 2, 6])
        mv0 = sb("mv0", [P, 2])
        mv1 = sb("mv1", [P, 2, 2])
        veps0 = sb("veps0", [P, 1])
        veps1 = sb("veps1", [P, 1])
        rstd0 = sb("rstd0", [P, 1])
        rstd1 = sb("rstd1", [P, 2])
        rfin = sb("rfin", [P, 2])
        nmax = sb("nmax", [P, 1])
        esum = sb("esum", [P, 1])
        erec = sb("erec", [P, 1])
        rmax = sb("rmax", [P, 1])
        rbias = sb("rbias", [P, 1])
        rsum = sb("rsum", [P, 1])
        rrec = sb("rrec", [P, 1])
        bank = [ctx.enter_context(nc.psum_tensor(f"bank{i}", [P, H], f32)) for i in range(8)]

        wk3 = wk_sb[:, :].rearrange("p (c d) -> p c d", c=CH)
        wq3 = wq_sb[:, :].rearrange("p (c d) -> p c d", c=CH)
        ctx_raw = wk_sb[:, 0:NB * CW].rearrange("p (b d) -> p b d", b=NB)
        scale_raw = wk_sb[:, NB * CW:NB * CW + 2 * D].rearrange("p (s d) -> p s d", s=2)
        bias_bc = wk_sb[:, NB * CW + 2 * D:NB * CW + 3 * D]
        junk = wk_sb[:, NB * CW + 3 * D:NB * CW + 3 * D + D // 2].bitcast(mybir.dt.bfloat16)
        x1b = wk_sb[:, 0:2 * D].rearrange("p (s d) -> p s d", s=2)
        os_sb = wq_sb[:, 0:2 * D].rearrange("p (s d) -> p s d", s=2)
        y_sb = wq_sb[:, 2 * D:4 * D].rearrange("p (s d) -> p s d", s=2)
        a_sb = wq_sb[:, 4 * D:5 * D]
        gw = w_stage[0:E, 0, :]
        gwT = w_stage[:, 1, :].rearrange("p (c w) -> p c w", c=CH)
        kqg4 = kqg[:, :].rearrange("p (b c w) -> p b c w", b=NB, c=CH)
        ctxs3 = ctxs[:, :].rearrange("p (b d) -> p b d", b=NB)

        gw_loaded = sem("gw_loaded")
        small_loaded = sem("small_loaded")
        ctxT_loaded = sem("ctxT_loaded")
        wq_means = sem("wq_means")
        gwT_zero = sem("gwT_zero")
        kqb_made = sem("kqb_made")
        kqb_ready = sem("kqb_ready")
        ssq0_ready = sem("ssq0_ready")
        gates_copied = sem("gates_copied")
        wk_loaded = [sem(f"wk_loaded{c}") for c in range(CH)]
        wq_loaded = [sem(f"wq_loaded{c}") for c in range(CH)]
        ctx_loaded = sem("ctx_loaded")
        scale_loaded = sem("scale_loaded")
        bias_loaded = sem("bias_loaded")
        w_loaded = [sem(f"w_loaded{s}") for s in range(2)]
        x_loaded = [sem(f"x_loaded{s}") for s in range(2)]
        xT_loaded = [sem(f"xT_loaded{s}") for s in range(2)]
        y_free = [sem(f"y_free{s}") for s in range(2)]
        consts = sem("consts")
        scale_zero = sem("scale_zero")
        gw_ready = sem("gw_ready")
        gwT_made = sem("gwT_made")
        gwT_ready = sem("gwT_ready")
        tanh_ready = sem("tanh_ready")
        k_made = sem("k_made")
        kT_act = sem("kT_act")
        kT_dve = sem("kT_dve")
        wq_centred = sem("wq_centred")
        kq_made = sem("kq_made")
        kq_act = sem("kq_act")
        kq_dve = sem("kq_dve")
        cacc_ready = sem("cacc_ready")
        cbias_made = sem("cbias_made")
        cbias_ready = sem("cbias_ready")
        cg_made = sem("cg_made")
        cg_ready = sem("cg_ready")
        ctx_hi = sem("ctx_hi")
        ctx_lo = sem("ctx_lo")
        scale_hi = sem("scale_hi")
        scale_lo = sem("scale_lo")
        sign_ready = sem("sign_ready")
        gb_ready = sem("gb_ready")
        act_steps = sem("act_steps")
        dve_steps = sem("dve_steps")
        pool_steps = sem("pool_steps")
        scores_made = sem("scores_made")
        rstd0_ready = sem("rstd0_ready")
        nmax_ready = sem("nmax_ready")
        exp_ready = sem("exp_ready")
        e2_ready = sem("e2_ready")
        attT_made = sem("attT_made")
        att_hi_ready = sem("att_hi_ready")
        att_lo_ready = sem("att_lo_ready")
        attended_made = sem("attended_made")
        x1_ready = sem("x1_ready")
        x1b_ready = sem("x1b_ready")
        veps1_ready = sem("veps1_ready")
        rstd1_ready = sem("rstd1_ready")
        rbias_ready = sem("rbias_ready")
        rexp_ready = sem("rexp_ready")
        route_ready = sem("route_ready")
        routeT_made = sem("routeT_made")
        route_hi = sem("route_hi")
        route_lo = sem("route_lo")
        is_made = sem("is_made")
        os_made = sem("os_made")
        os_ready = sem("os_ready")
        a_ready = sem("a_ready")
        aT_made = sem("aT_made")
        aT_hi_ready = sem("aT_hi_ready")
        aT_lo_ready = sem("aT_lo_ready")
        ffn_made = sem("ffn_made")
        scaled_ready = sem("scaled_ready")
        y_ready = sem("y_ready")

        block = ctx.enter_context(nc.Block())

        def half(h):
            return slice(h * H, (h + 1) * H)

        def pairs(eng, steps, per_pair, iteration):
            with eng.Fori(0, (NT - 4) // 2) as i:
                if steps is not None:
                    start, steps.loop = steps.count, i * per_pair
                for c in range(2):
                    iteration(2 * i + (2 + c), c, (2 * i + (3 + c)) // TPB)
                if steps is not None:
                    assert steps.count - start == per_pair, steps.count - start
                    steps.loop, steps.count = 0, start + per_pair * ((NT - 4) // 2)

        @block.sync
        def _(sp):
            sp.dma_start(gw, gate_w).then_inc(gw_loaded, 16)
            sp.dma_start(ctxT[:, :, :], ctx_cols).then_inc(ctxT_loaded, 16)
            for c in range(CH):
                sp.dma_start(wk3[:, c, :], wk_cols[c * P:(c + 1) * P, :]).then_inc(wk_loaded[c], 16)
            for c in range(CH):
                sp.dma_start(wq3[:, c, :], wq_rows[c * P:(c + 1) * P, :]).then_inc(wq_loaded[c], 16)

            def load(t, s):
                sp.dma_start(xT_sb[:, s, :, :], x_cols[bass.ds(t * P, P), :, :]).then_inc(xT_loaded[s], 16)
                sp.dma_start(x_sb[:, s, :], x_rows[bass.ds(t * P, P), :]).then_inc(x_loaded[s], 16)

            for t in range(2):
                load(t, t)
            sp.wait_ge(k_made, CH)
            for d in range(2):
                sp.dma_start(ctx_raw[d * NC:(d + 1) * NC, :, 0:D], ctx_rows.rearrange("b p d -> p b d"))\
                  .then_inc(ctx_loaded, 16)
            sp.dma_start(bias_bc, ffn_bias.rearrange("(a n) -> a n", a=1).to_broadcast([P, D])).then_inc(bias_loaded, 16)
            sp.wait_ge(scale_zero, 1)
            for g in range(4):
                for n, src in enumerate((in_scale, out_scale)):
                    sp.dma_start(scale_raw[g * GRP:g * GRP + E, n, :], src).then_inc(scale_loaded, 16)
            for c in range(CH):
                if c >= 2:
                    sp.wait_ge(sign_ready, c - 1)
                sp.dma_start(w_stage[:, c % 2, :], w_cols[c * P:(c + 1) * P, :]).then_inc(w_loaded[c % 2], 16)

            def load_into_used(t, s):
                sp.wait_ge(scores_made, t - 1)
                sp.wait_ge(x1_ready, t - 1)
                load(t, s)

            def store(t, s):
                sp.wait_ge(y_ready, 2 * t + 2)
                sp.dma_start(y_rows[bass.ds(t * P, P), :], y_sb[:, s, :]).then_inc(y_free[s], 16)

            sp.wait_ge(kqb_made, CH)
            for s in range(2):
                sp.sem_inc(y_free[s], 16)
            for t in (2, 3):
                load_into_used(t, t % 2)
            with sp.Fori(0, (NT - 4) // 2) as i:
                for c in range(2):
                    store(2 * i + c, c)
                    load_into_used(2 * i + (4 + c), c)
            for t in range(NT - 4, NT):
                store(t, t % 2)
            for s in range(2):
                sp.wait_ge(y_free[s], 16 * (NT // 2) + 16)

        @block.gpsimd
        def _(pool):
            steps = Steps(pool, pool_steps)
            steps.done(nc.gpsimd.memset(ident[:, :], 0.0))
            nc.gpsimd.memset(gwT, 0.0).then_inc(gwT_zero, 1)
            nc.gpsimd.memset(ones[:, :], 1.0)
            nc.gpsimd.memset(eps_d[:, :], EPS * D)
            nc.gpsimd.memset(neg_half[:, :], -0.5)
            nc.gpsimd.memset(route[:, :, :], 0.0)
            nc.gpsimd.memset(kqg4[:, :, :, NC + E:KW], 0.0)
            steps.wait()
            nc.gpsimd.affine_select(out=ident[:, :], in_=ident[:, :], compare_op=ALU.not_equal, fill=1.0, base=0,
                                    pattern=[[-1, P]], channel_multiplier=1).then_inc(consts, 1)
            pool.wait_ge(k_made, CH)
            nc.gpsimd.memset(scale_raw, 0.0).then_inc(scale_zero, 1)

            def x_rstd(t):
                pool.wait_ge(ssq0_ready, t + 1)
                steps.done(nc.gpsimd.tensor_tensor(veps0[:, :], ssq0[:, :], eps_d[:, :], ALU.add))
                steps.wait()
                nc.gpsimd.tensor_tensor(rstd0[:, :], veps0[:, :], neg_half[:, :], ALU.pow).then_inc(rstd0_ready, 1)

            def iteration(j, s, b=None, prev=True, cur=True, nxt=True):
                def add_up(h):
                    if h == 0:
                        pool.wait_ge(x1b_ready, j)
                    pool.wait_ge(scaled_ready, 2 * j + (h - 1))
                    nc.gpsimd.tensor_tensor(y_sb[:, 1 - s, half(h)], y_sb[:, 1 - s, half(h)],
                                            x1b[:, 1 - s, half(h)], ALU.add).then_inc(y_ready, 1)

                if prev:
                    add_up(0)
                    add_up(1)
                if nxt and not (isinstance(j, int) and j + 2 >= NT):
                    x_rstd(j + 2)
                if nxt:
                    pool.wait_ge(veps1_ready, j + 2)
                    nc.gpsimd.tensor_tensor(rstd1[:, 1 - s:2 - s], veps1[:, :], neg_half[:, :], ALU.pow)\
                      .then_inc(rstd1_ready, 1)
                    if prev:
                        pool.wait_ge(y_ready, 2 * j)
                    nc.gpsimd.tensor_tensor(x1b[:, 1 - s, :], x1[:, 1 - s, :], bias_bc, ALU.add).then_inc(x1b_ready, 1)

            x_rstd(0)
            pool.wait_ge(gb_ready, 1)
            iteration(-1, 1, prev=False, cur=False)
            iteration(0, 0, prev=False)
            iteration(1, 1)
            pairs(pool, steps, 2, iteration)
            iteration(NT - 2, 0)
            iteration(NT - 1, 1, nxt=False)
            iteration(NT, 0, cur=False, nxt=False)

        @block.scalar
        def _(act):
            act.dma_start(bqT[:, :], bq_cols).then_inc(small_loaded, 16)
            act.dma_start(bkT[:, :], bk_cols).then_inc(small_loaded, 16)
            act.dma_start(gates[:, 0:1], g_xattn.rearrange("(a n) -> a n", a=1).to_broadcast([P, 1])).then_inc(small_loaded, 16)
            act.dma_start(gates[:, 1:2], g_ffn.rearrange("(a n) -> a n", a=1).to_broadcast([P, 1])).then_inc(small_loaded, 16)
            steps = Steps(act, act_steps)
            for c in range(CH):
                act.wait_ge(wq_loaded[c], 16)
                nc.scalar.activation(signT[:, c, :], wq3[:, c, :], ACT.Copy, scale=1.0 / D,
                                     accum_out=wq_mean[:, c:c + 1]).then_inc(wq_means, 1)
            act.wait_ge(small_loaded, 64)
            nc.scalar.activation(tgates[:, :], gates[:, :], ACT.Tanh).then_inc(tanh_ready, 1)
            for c in range(0, CH, 2):
                act.wait_ge(k_made, c + 1)
                nc.scalar.activation(kT[:, c, :], bank[c][:, 0:CTX], ACT.Identity, bias=bkT[:, c:c + 1]).then_inc(kT_act, 1)

            def context_high(b):
                nc.scalar.activation(ctxs3[:, b, :], ctx_raw[:, b, :], ACT.Copy).then_inc(ctx_hi, 1)

            def signs(chunks):
                for n in chunks:
                    act.wait_ge(w_loaded[n % 2], 16 * (n // 2 + 1))
                    nc.scalar.activation(signT[:, n, :], w_stage[:, n % 2, :], ACT.Sign).then_inc(sign_ready, 1)

            def kq_out(m, first, made, ready):
                act.wait_ge(made, m + 1)
                src = bank[m if first == 0 else 3 + m % 4][:, 0:2 * NC].rearrange("p (b n) -> p b n", b=2)
                nc.scalar.activation(kqg4[:, first:first + 2, m, 0:NC], src, ACT.Copy).then_inc(ready, 1)

            act.wait_ge(ctx_loaded, 32)
            act.wait_ge(gates_copied, 1)
            context_high(0)
            kq_out(0, 0, kq_made, kq_act)
            signs(range(0, 1))
            context_high(1)
            kq_out(2, 0, kq_made, kq_act)
            signs(range(1, 3))
            kq_out(4, 0, kq_made, kq_act)
            act.wait_ge(scale_loaded, 16 * 8)
            nc.scalar.activation(scales[:, :, :], scale_raw, ACT.Copy).then_inc(scale_hi, 1)
            act.wait_ge(cbias_made, 1)
            nc.scalar.activation(cbias[:, :], bank[7][:, 0:CTX], ACT.Copy, scale=SC).then_inc(cbias_ready, 1)
            kq_out(6, 0, kq_made, kq_act)
            signs(range(3, 4))
            context_high(2)
            context_high(3)

            def x_statistics(t, s):
                act.wait_ge(x_loaded[s], 16 * (t // 2) + 16)
                steps.done(nc.scalar.activation(junk, x_sb[:, s, :], ACT.Copy, scale=-1.0 / D,
                                                accum_out=nmean0[:, 0:1]))
                steps.wait()
                nc.scalar.activation(junk, x_sb[:, s, :], ACT.Square, bias=nmean0[:, 0:1],
                                     accum_out=ssq0[:, 0:1]).then_inc(ssq0_ready, 1)

            x_statistics(0, 0)

            def iteration(j, s, b=None, prev=True, cur=True, nxt=True, kqb=False):
                if cur:
                    act.wait_ge(routeT_made, j + 1)
                    nc.scalar.activation(routeT[:, :], bank[2][:, 0:P], ACT.Copy).then_inc(route_hi, 1)
                if nxt:
                    act.wait_ge(nmax_ready, j + 2)
                    nc.scalar.activation(e_sb[:, :], s_sb[:, :], ACT.Exp, bias=nmax[:, 0:1],
                                         accum_out=esum[:, 0:1]).then_inc(exp_ready, 1)
                if kqb:
                    for m in range(0, 4):
                        kq_out(m, 2, kqb_made, kqb_ready)
                if cur:
                    for h in range(2):
                        act.wait_ge(os_made, 2 * j + (h + 1))
                        nc.scalar.activation(os_sb[:, s, half(h)], bank[h][:, :], ACT.Copy).then_inc(os_ready, 1)
                if nxt:
                    act.wait_ge(attT_made, j + 2)
                    nc.scalar.activation(att_hi[:, :], bank[7][:, 0:P], ACT.Copy).then_inc(att_hi_ready, 1)
                if cur:
                    for h in range(2):
                        act.wait_ge(aT_made, 2 * j + (h + 1))
                        nc.scalar.activation(aT_hi[:, s, h * CH // 2:(h + 1) * CH // 2, :],
                                             bank[3 + h][:, :].rearrange("p (c t) -> p c t", t=P), ACT.Copy)\
                          .then_inc(aT_hi_ready, 1)
                if kqb:
                    signs(range(4, CH))
                if nxt and not (isinstance(j, int) and j + 2 >= NT):
                    x_statistics(j + 2, s)
                if kqb:
                    for m in range(4, CH):
                        kq_out(m, 2, kqb_made, kqb_ready)
                if nxt:
                    act.wait_ge(rbias_ready, j + 2)
                    nc.scalar.activation(eroute[:, :], logit[:, :], ACT.Exp, bias=rbias[:, 0:1],
                                         scale=rstd1[:, 1 - s:2 - s], accum_out=rsum[:, 0:1]).then_inc(rexp_ready, 1)

            iteration(-1, 1, prev=False, cur=False, kqb=True)
            iteration(0, 0, prev=False)
            iteration(1, 1)
            pairs(act, steps, 2, iteration)
            iteration(NT - 2, 0)
            iteration(NT - 1, 1, nxt=False)

        @block.vector
        def _(dve):
            steps = Steps(dve, dve_steps)

            def mean_var(src, out):
                for h in range(2):
                    last = nc.vector.bn_stats(st[0:src.shape[0], h, :], src[:, half(h)])
                steps.done(last)
                steps.wait()
                nc.vector.memset(hold[:, :], 0.0)
                steps.done(nc.vector.bn_aggr(out, st[0:src.shape[0], :, :]))
                steps.wait()

            dve.wait_ge(gw_loaded, 16)
            mean_var(gw, mv0[0:E, :])
            nc.vector.tensor_scalar(gw, gw, mv0[0:E, 0:1], None, ALU.subtract).then_inc(gw_ready, 1)
            dve.wait_ge(gwT_zero, 1)
            dve.wait_ge(gwT_made, 1)
            turned = bank[7][:, 0:CH * E].rearrange("p (c e) -> p c e", e=E)
            nc.vector.tensor_copy(gwT[:, :, 0:E], turned).then_inc(gwT_ready, 1)
            for b in range(NB):
                last = nc.vector.tensor_copy(kqg4[:, b, :, NC:NC + E], turned)
            last.then_inc(gwT_ready, 1)
            dve.wait_ge(cg_made, 1)
            for m in range(CTX // P):
                last = nc.vector.tensor_copy(cgs[:, m, :], bank[5 + m][:, 0:E])
            last.then_inc(cg_ready, 1)
            for c in range(CH):
                dve.wait_ge(wq_means, c + 1)
                nc.vector.tensor_scalar(wq3[:, c, :], wq3[:, c, :], wq_mean[:, c:c + 1], None, ALU.subtract).then_inc(wq_centred, 1)
            dve.wait_ge(small_loaded, 64)
            for c in range(1, CH, 2):
                dve.wait_ge(k_made, c + 1)
                nc.vector.tensor_scalar(kT[:, c, :], bank[c][:, 0:CTX], bkT[:, c:c + 1], None, ALU.add).then_inc(kT_dve, 1)
            dve.wait_ge(cg_ready, 1)
            for b in range(NB):
                rows = slice((b % 2) * NC, (b % 2 + 1) * NC)
                for d in range(2):
                    last = nc.vector.tensor_copy(ctx_raw[d * NC:(d + 1) * NC, b, D:CW], cgs[rows, b // 2, :])
            last.then_inc(gates_copied, 1)
            dve.wait_ge(kT_dve, CH // 2)
            dve.wait_ge(kT_act, CH // 2)
            for c in range(CH):
                if c == 0:
                    ins = nc.vector.tensor_scalar(cacc[:, :], kT[:, c, :], bqT[:, c:c + 1], None, ALU.mult)
                else:
                    ins = nc.vector.scalar_tensor_tensor(out=cacc[:, :], in0=kT[:, c, :], scalar=bqT[:, c:c + 1],
                                                         in1=cacc[:, :], op0=ALU.mult, op1=ALU.add)
                if c == CH - 1:
                    ins.then_inc(cacc_ready, 1)
                else:
                    steps.done(ins)
                    steps.wait()
            def context_low(b):
                dve.wait_ge(ctx_hi, b + 1)
                nc.vector.tensor_tensor(ctxs3[NC:P, b, :], ctx_raw[NC:P, b, :], ctxs3[NC:P, b, :].bitcast(f32),
                                        ALU.subtract).then_inc(ctx_lo, 1)

            def kq_out(m):
                dve.wait_ge(kq_made, m + 1)
                nc.vector.tensor_copy(kqg4[:, 0:2, m, 0:NC], bank[m][:, 0:2 * NC].rearrange("p (b n) -> p b n", b=2))\
                  .then_inc(kq_dve, 1)

            kq_out(1)
            context_low(0)
            kq_out(3)
            context_low(1)
            kq_out(5)
            dve.wait_ge(bias_loaded, 16)
            dve.wait_ge(tanh_ready, 1)
            nc.vector.tensor_scalar(bias_bc, bias_bc, tgates[:, 1:2], None, ALU.mult).then_inc(gb_ready, 1)
            kq_out(7)
            context_low(2)
            context_low(3)

            def iteration(j, s, b=None, prev=True, cur=True, nxt=True, scale_parts=False):
                n = 1 - s

                def scale_output(h):
                    dve.wait_ge(ffn_made, 2 * j + (h - 1))
                    nc.vector.scalar_tensor_tensor(out=y_sb[:, n, half(h)], in0=bank[5 + h][:, :],
                                                   scalar=rfin[:, n:n + 1], in1=os_sb[:, n, half(h)],
                                                   op0=ALU.mult, op1=ALU.mult).then_inc(scaled_ready, 1)

                def low_half(h):
                    dve.wait_ge(aT_hi_ready, 2 * j + (h + 1))
                    chunks = slice(h * CH // 2, (h + 1) * CH // 2)
                    nc.vector.tensor_tensor(aT_lo[:, s, chunks, :], bank[3 + h][:, :].rearrange("p (c t) -> p c t", t=P),
                                            aT_hi[:, s, chunks, :].bitcast(f32), ALU.subtract).then_inc(aT_lo_ready, 1)

                if prev:
                    dve.wait_ge(y_free[n], 16 * ((j - 1) // 2) + 16)
                    scale_output(0)
                if cur:
                    dve.wait_ge(route_hi, j + 1)
                    nc.vector.tensor_tensor(routeT[NC:P, :], bank[2][NC:P, 0:P], routeT[NC:P, :].bitcast(f32),
                                            ALU.subtract).then_inc(route_lo, 1)
                if nxt:
                    dve.wait_ge(scores_made, j + 2)
                    dve.wait_ge(rstd0_ready, j + 2)
                    steps.done(nc.vector.scalar_tensor_tensor(
                        out=s_sb[:, :], in0=bank[7][:, 0:NC], scalar=rstd0[:, 0:1],
                        in1=cbias[:, bass.ds(b * NC, NC)], op0=ALU.mult, op1=ALU.add))
                    nc.vector.tensor_copy(xgate[:, n, :], bank[7][:, NC:NC + E])
                    steps.wait()
                    nc.vector.reduce_max(nmax[:, :], s_sb[:, :], AX.X, negate=True).then_inc(nmax_ready, 1)
                    dve.wait_ge(exp_ready, j + 2)
                    steps.done(nc.vector.reciprocal(erec[:, :], esum[:, :]))
                    steps.wait()
                    nc.vector.tensor_scalar(e2[:, :, :], e_sb[:, :].unsqueeze(1).to_broadcast([P, 2, NC]),
                                            erec[:, 0:1], tgates[:, 0:1], ALU.mult, ALU.mult).then_inc(e2_ready, 1)
                if cur:
                    for h in range(2):
                        dve.wait_ge(is_made, 2 * j + (h + 1))
                        nc.vector.scalar_tensor_tensor(out=a_sb[:, half(h)], in0=x1[:, s, half(h)],
                                                       scalar=mv1[:, s, 0:1], in1=bank[3 + h][:, :],
                                                       op0=ALU.subtract, op1=ALU.mult).then_inc(a_ready, 1)
                if nxt:
                    dve.wait_ge(att_hi_ready, j + 2)
                    nc.vector.tensor_tensor(att_lo[:, :], bank[7][:, 0:P], att_hi[:, :].bitcast(f32),
                                            ALU.subtract).then_inc(att_lo_ready, 1)
                if prev:
                    scale_output(1)
                if scale_parts:
                    dve.wait_ge(scale_hi, 1)
                    for g in (1, 3):
                        rows = slice(g * GRP, (g + 1) * GRP)
                        nc.vector.tensor_tensor(scales[rows, :, :], scale_raw[rows, :, :], scales[rows, :, :].bitcast(f32),
                                                ALU.subtract).then_inc(scale_lo, 1)
                if cur:
                    low_half(0)
                    low_half(1)
                if nxt:
                    dve.wait_ge(attended_made, j + 2)
                    if not (isinstance(j, int) and j < 1):
                        dve.wait_ge(x1b_ready, j)
                    for i in range(3):
                        cols = slice(i * AW, min((i + 1) * AW, D))
                        last = nc.vector.tensor_tensor(x1[:, n, cols], x_sb[:, n, cols],
                                                       bank[i][:, 0:cols.stop - cols.start], ALU.add)
                    last.then_inc(x1_ready, 1)
                    steps.done(nc.vector.tensor_tensor(logit[:, :], xgate[:, n, :], bank[2][:, D - 2 * AW:AW], ALU.add))
                    steps.wait()
                    nc.vector.reduce_max(rmax[:, :], logit[:, :], AX.X, negate=True)
                    mean_var(x1[:, n, :], mv1[:, n, :])
                    nc.vector.tensor_scalar(veps1[:, :], mv1[:, n, 1:2], EPS, None, ALU.add).then_inc(veps1_ready, 1)
                    dve.wait_ge(rstd1_ready, j + 2)
                    nc.vector.tensor_scalar(rbias[:, :], rmax[:, :], rstd1[:, n:n + 1], None, ALU.mult)\
                      .then_inc(rbias_ready, 1)
                    nc.vector.tensor_scalar(rfin[:, n:n + 1], rstd1[:, n:n + 1], tgates[:, 1:2], None, ALU.mult)
                    dve.wait_ge(rexp_ready, j + 2)
                    steps.done(nc.vector.reciprocal(rrec[:, :], rsum[:, :]))
                    steps.wait()
                    nc.vector.tensor_scalar(route[:, :, 0:E], eroute[:, :].unsqueeze(1).to_broadcast([P, 4, E]),
                                            rrec[:, 0:1], None, ALU.mult).then_inc(route_ready, 1)

            dve.wait_ge(cbias_ready, 1)
            iteration(-1, 1, 0, prev=False, cur=False, scale_parts=True)
            iteration(0, 0, 0, prev=False)
            iteration(1, 1, 0)
            pairs(dve, steps, 2 * 6, iteration)
            iteration(NT - 2, 0, NB - 1)
            iteration(NT - 1, 1, nxt=False)
            iteration(NT, 0, cur=False, nxt=False)

        @block.tensor
        def _(pe):
            pe.wait_ge(consts, 1)
            pe.wait_ge(gw_ready, 1)
            for c in range(CH):
                last = nc.tensor.transpose(bank[7][:, c * E:(c + 1) * E], gw[:, c * P:(c + 1) * P], ident[0:E, 0:E])
            last.then_inc(gwT_made, 1)
            pe.wait_ge(ctxT_loaded, 16)
            pe.wait_ge(gwT_ready, 1)
            for m in range(CTX // P):
                for c in range(CH):
                    last = nc.tensor.matmul(bank[5 + m][:, 0:KW], ctxT[:, c, m * P:(m + 1) * P], gwT[:, c, :],
                                            start=(c == 0), stop=(c == CH - 1))
            last.then_inc(cg_made, 1)
            for c in range(CH):
                pe.wait_ge(wk_loaded[c], 16)
                for m in range(CH):
                    if c == 0 and m == 5:
                        pe.wait_ge(cg_ready, 1)
                    if c == 0 and m == 7:
                        pe.wait_ge(gwT_ready, 2)
                    last = nc.tensor.matmul(bank[m][:, 0:CTX], wk3[:, c, m * P:(m + 1) * P], ctxT[:, c, :],
                                            start=(c == 0), stop=(c == CH - 1))
                    if c == CH - 1:
                        last.then_inc(k_made, 1)

            def kq(out, m, first, made):
                for c in range(CH):
                    last = nc.tensor.matmul(out[:, 0:2 * NC], wq3[:, c, m * P:(m + 1) * P],
                                            kT[:, c, first * NC:(first + 2) * NC], start=(c == 0), stop=(c == CH - 1))
                last.then_inc(made, 1)

            pe.wait_ge(kT_act, CH // 2)
            pe.wait_ge(kT_dve, CH // 2)
            pe.wait_ge(wq_centred, CH)
            for m in range(CH):
                if m == 6:
                    pe.wait_ge(cacc_ready, 1)
                    nc.tensor.matmul(bank[7][:, 0:CTX], ones[:, :], cacc[:, :], start=True, stop=True)\
                      .then_inc(cbias_made, 1)
                if m == 7:
                    pe.wait_ge(cbias_ready, 1)
                kq(bank[m], m, 0, kq_made)

            def kq_later(m):
                if m >= 4:
                    pe.wait_ge(kqb_ready, m - 3)
                kq(bank[3 + m % 4], m, 2, kqb_made)

            def ffn(t, s, quarters):
                for q in quarters:
                    h, part = q // 4, q % 4 // 2
                    if q % 4 == 0 and not (isinstance(t, int) and t < 1):
                        pe.wait_ge(scaled_ready, 2 * t + (h - 1))
                    if q < 2:
                        pe.wait_ge(aT_hi_ready, 2 * t + (q + 1))
                    if q == 2:
                        pe.wait_ge(aT_lo_ready, 2 * t + 2)
                    src = (aT_hi, aT_lo)[part]
                    for c in range(q % 2 * 4, q % 2 * 4 + 4):
                        last = nc.tensor.matmul(bank[5 + h][:, :], src[:, s, c, :], signT[:, c, half(h)],
                                                start=(part == 0 and c == 0), stop=(part == 1 and c == CH - 1))
                    if q % 4 == 3:
                        last.then_inc(ffn_made, 1)

            def iteration(j, s, b=None, prev=True, cur=True, nxt=True, kqb=False):
                n = 1 - s
                if prev:
                    ffn(j - 1, n, range(4))
                if nxt:
                    pe.wait_ge(xT_loaded[n], 16 * ((j + 1) // 2) + 16)
                    for c in range(CH):
                        last = nc.tensor.matmul(bank[7][:, 0:KW], xT_sb[:, n, c, :],
                                                kqg[:, bass.ds(b * (CH * KW) + c * KW, KW)],
                                                start=(c == 0), stop=(c == CH - 1))
                    last.then_inc(scores_made, 1)
                if cur:
                    pe.wait_ge(route_ready, j + 1)
                    nc.tensor.transpose(bank[2][:, 0:P], route[:, :, :].rearrange("p g e -> p (g e)"), ident[:, :])\
                      .then_inc(routeT_made, 1)
                if prev:
                    ffn(j - 1, n, range(4, 6))
                if cur:
                    pe.wait_ge(route_hi, j + 1)
                    pe.wait_ge(route_lo, j + 1)
                    for k, first, made in ((0, 3, is_made), (1, 0, os_made)):
                        for h in range(2):
                            nc.tensor.matmul(bank[first + h][:, :], routeT[:, :], scales[:, k, half(h)],
                                             start=True, stop=True).then_inc(made, 1)
                if kqb:
                    kq_later(0)
                    kq_later(1)
                if nxt:
                    pe.wait_ge(e2_ready, j + 2)
                    nc.tensor.transpose(bank[7][:, 0:P], e2[:, :, :].rearrange("p a n -> p (a n)"), ident[:, :])\
                      .then_inc(attT_made, 1)
                if kqb:
                    kq_later(2)
                    kq_later(3)
                if prev:
                    ffn(j - 1, n, range(6, 8))
                if cur:
                    for h in range(2):
                        pe.wait_ge(a_ready, 2 * j + (h + 1))
                        for c in range(CH // 2):
                            k = h * CH // 2 + c
                            last = nc.tensor.transpose(bank[3 + h][:, c * P:(c + 1) * P], a_sb[:, k * P:(k + 1) * P],
                                                       ident[:, :])
                        last.then_inc(aT_made, 1)
                if nxt:
                    pe.wait_ge(att_hi_ready, j + 2)
                    pe.wait_ge(att_lo_ready, j + 2)
                    if not (isinstance(j, int) and j < 0):
                        pe.wait_ge(os_ready, 2 * j + 2)
                    for i in range(3):
                        for part, src in enumerate((att_hi, att_lo)):
                            last = nc.tensor.matmul(bank[i][:, 0:AW], src[:, :], ctxs[:, bass.ds(b * CW + i * AW, AW)],
                                                    start=(part == 0), stop=(part == 1))
                    last.then_inc(attended_made, 1)
                if kqb:
                    for m in range(4, CH):
                        kq_later(m)

            pe.wait_ge(kq_act, CH // 2)
            pe.wait_ge(kq_dve, CH // 2)
            pe.wait_ge(ctx_lo, 1)
            iteration(-1, 1, 0, prev=False, cur=False, kqb=True)
            pe.wait_ge(scale_lo, 2)
            pe.wait_ge(kqb_ready, CH)
            pe.wait_ge(ctx_lo, NB)
            iteration(0, 0, 0, prev=False)
            pe.wait_ge(sign_ready, CH)
            iteration(1, 1, 0)
            pairs(pe, None, 0, iteration)
            iteration(NT - 2, 0, NB - 1)
            iteration(NT - 1, 1, nxt=False)
            iteration(NT, 0, cur=False, nxt=False)


def kernel(**inputs):
    import numpy as np
    import concourse.bacc as bacc
    from concourse.bass_utils import run_bass_kernel_spmd

    P = 128
    a = {k: np.asarray(v) for k, v in inputs.items()}
    x = a["x"].reshape(-1, a["x"].shape[-1])
    T, D = x.shape
    CH = D // P
    ctx = a["ctx_4096"]

    def columns(v):
        return v.reshape(CH, P, -1).transpose(1, 0, 2)

    arrays = {
        "x_rows": x,
        "x_cols": x.reshape(T // P, P, CH, P).transpose(0, 3, 2, 1).reshape(T, CH, P),
        "ctx_rows": ctx,
        "ctx_cols": columns(ctx.reshape(-1, D).T),
        "g_xattn": a["g_xattn"],
        "g_ffn": a["g_ffn"],
        "wq_rows": a["L0_xattn_Wq"],
        "bq_cols": columns(a["L0_xattn_bq"][:, None])[:, :, 0],
        "wk_cols": a["L0_xattn_Wk"].T,
        "bk_cols": columns(a["L0_xattn_bk"][:, None])[:, :, 0],
        "w_cols": a["L0_ffn_weight"].T,
        "ffn_bias": a["L0_ffn_bias"],
        "gate_w": a["L0_ffn_gate_w"],
        "in_scale": a["L0_ffn_in_channel_scale"],
        "out_scale": a["L0_ffn_out_channel_scale"],
    }
    nc = bacc.Bacc("TRN2", target_bir_lowering=False, num_devices=1)
    feeds, args = {}, []
    for name, v in arrays.items():
        v = np.ascontiguousarray(v)
        feeds[f"in_{name}"] = v
        args.append(nc.dram_tensor(f"in_{name}", v.shape, mybir.dt.from_np(v.dtype), kind="ExternalInput").ap())
    args.append(nc.dram_tensor("out_y", (T, D), mybir.dt.float32, kind="ExternalOutput").ap())
    gated_cross_attention_and_routed_ffn(nc, *args)
    r = run_bass_kernel_spmd(nc, [feeds], core_ids=[0])
    return r.results[0]["out_y"].reshape(a["x"].shape)
```

```python
import concourse.bass as bass
from concourse import mybir
from contextlib import ExitStack


class Steps:

    def __init__(self, eng, sem):
        self.eng, self.sem, self.count, self.loop = eng, sem, 0, 0

    def done(self, instruction):
        instruction.then_inc(self.sem, 1)
        self.count += 1

    def wait(self):
        self.eng.wait_ge(self.sem, self.loop + self.count)


def gated_cross_attention_and_routed_ffn(nc, x_rows, x_cols, ctx_rows, ctx_cols, g_xattn, g_ffn, wq_rows, bq_cols,
                                         wk_cols, bk_cols, w_cols, ffn_bias, gate_w, in_scale, out_scale, y_rows):
    f32, f32r = mybir.dt.float32, mybir.dt.float32r
    ALU, ACT, AX = mybir.AluOpType, mybir.ActivationFunctionType, mybir.AxisListType

    P = 128
    T, D = x_rows.shape
    NB, NC = ctx_rows.shape[0], ctx_rows.shape[1]
    E = gate_w.shape[0]
    CH = D // P
    NT = T // P
    TPB = NT // NB
    H = D // 2
    CW = D + E
    AW = CW // 3
    KW = P
    EPS = 1e-5
    SC = float(D) ** -0.5
    CTX = NB * NC
    WARM = 7
    LATER = (3, 4, 5, 6, 3, 5, 6, 5)
    GRP = 32

    ctx = ExitStack()
    with ctx:
        def sb(name, shape, dt=f32):
            return ctx.enter_context(nc.sbuf_tensor(name, shape, dt))

        def sem(name):
            return ctx.enter_context(nc.semaphore(name))

        wk_sb = sb("wk_sb", [P, CH * D])
        wq_sb = sb("wq_sb", [P, CH * D])
        ctxT = sb("ctxT", [P, CH, CTX])
        kT = sb("kT", [P, CH, CTX])
        kqg = sb("kqg", [P, NB * CH * KW])
        signT = sb("signT", [P, CH, D], f32r)
        w_stage = sb("w_stage", [P, 2, D])
        ctxs = sb("ctxs", [P, NB * CW], f32r)
        scales = sb("scales", [P, 2, D], f32r)
        x_sb = sb("x_sb", [P, 2, D])
        xT_sb = sb("xT_sb", [P, 2, CH, P])
        x1 = sb("x1", [P, 2, D])
        aT_hi = sb("aT_hi", [P, 2, CH, P], f32r)
        aT_lo = sb("aT_lo", [P, 2, CH, P], f32r)
        ident = sb("ident", [P, P])
        ones = sb("ones", [P, P])
        cbias = sb("cbias", [P, CTX])
        cacc = sb("cacc", [P, CTX])
        cgs = sb("cgs", [P, CTX // P, E])
        wq_mean = sb("wq_mean", [P, CH])
        nmean0 = sb("nmean0", [P, 1])
        ssq0 = sb("ssq0", [P, 1])
        eps_d = sb("eps_d", [P, 1])
        bqT = sb("bqT", [P, CH])
        bkT = sb("bkT", [P, CH])
        gates = sb("gates", [P, 2])
        tgates = sb("tgates", [P, 2])
        att_hi = sb("att_hi", [P, P], f32r)
        att_lo = sb("att_lo", [P, P], f32r)
        s_sb = sb("s_sb", [P, NC])
        e_sb = sb("e_sb", [P, NC])
        e2 = sb("e2", [P, 2, NC])
        route = sb("route", [P, 4, GRP])
        routeT = sb("routeT", [P, P], f32r)
        xgate = sb("xgate", [P, 2, E])
        logit = sb("logit", [P, E])
        eroute = sb("eroute", [P, E])
        hold = sb("hold", [P, 1])
        neg_half = sb("neg_half", [P, 1])
        st = sb("st", [P, 2, 6])
        mv0 = sb("mv0", [P, 2])
        mv1 = sb("mv1", [P, 2, 2])
        veps0 = sb("veps0", [P, 1])
        veps1 = sb("veps1", [P, 1])
        rstd0 = sb("rstd0", [P, 1])
        rstd1 = sb("rstd1", [P, 2])
        rfin = sb("rfin", [P, 2])
        nmax = sb("nmax", [P, 1])
        esum = sb("esum", [P, 1])
        erec = sb("erec", [P, 1])
        rmax = sb("rmax", [P, 1])
        rbias = sb("rbias", [P, 1])
        rsum = sb("rsum", [P, 1])
        rrec = sb("rrec", [P, 1])
        bank = [ctx.enter_context(nc.psum_tensor(f"bank{i}", [P, H], f32)) for i in range(8)]

        wk3 = wk_sb[:, :].rearrange("p (c d) -> p c d", c=CH)
        wq3 = wq_sb[:, :].rearrange("p (c d) -> p c d", c=CH)
        ctx_raw = wk_sb[:, 0:NB * CW].rearrange("p (b d) -> p b d", b=NB)
        scale_raw = wk_sb[:, NB * CW:NB * CW + 2 * D].rearrange("p (s d) -> p s d", s=2)
        bias_bc = wk_sb[:, NB * CW + 2 * D:NB * CW + 3 * D]
        junk = wk_sb[:, NB * CW + 3 * D:NB * CW + 3 * D + D // 2].bitcast(mybir.dt.bfloat16)
        x1b = wk_sb[:, 0:2 * D].rearrange("p (s d) -> p s d", s=2)
        a_sb = wk_sb[:, 2 * D:3 * D]
        os_sb = scale_raw
        y_sb = wq_sb[:, 0:2 * D].rearrange("p (s d) -> p s d", s=2)
        gw = x1[0:E, 1, :]
        w_raw = [buf[:, c, :] for buf in (w_stage, x1, w_stage, w_stage) for c in range(2)]
        kqg4 = kqg[:, :].rearrange("p (b c w) -> p b c w", b=NB, c=CH)
        gwT = kqg4[:, NB - 1, :, :]
        ctxs3 = ctxs[:, :].rearrange("p (b d) -> p b d", b=NB)

        gw_loaded = sem("gw_loaded")
        small_loaded = sem("small_loaded")
        ctxT_loaded = [sem(f"ctxT_loaded{c}") for c in range(CH)]
        wq_means = sem("wq_means")
        gwT_zero = sem("gwT_zero")
        kq_later_made = sem("kq_later_made")
        kq_later_ready = sem("kq_later_ready")
        ssq0_ready = sem("ssq0_ready")
        gates_copied = sem("gates_copied")
        wk0_loaded = sem("wk0_loaded")
        ones_ready = sem("ones_ready")
        wk_loaded = [sem(f"wk_loaded{c}") for c in range(CH)]
        wq_loaded = [sem(f"wq_loaded{c}") for c in range(CH)]
        ctx_loaded = [sem(f"ctx_loaded{i}") for i in range(2)]
        scale_loaded = sem("scale_loaded")
        bias_loaded = sem("bias_loaded")
        w_loaded = [sem(f"w_loaded{c}") for c in range(CH)]
        x_loaded = [sem(f"x_loaded{s}") for s in range(2)]
        xT_loaded = [sem(f"xT_loaded{s}") for s in range(2)]
        y_free = [sem(f"y_free{s}") for s in range(2)]
        consts = sem("consts")
        scale_zero = sem("scale_zero")
        gw_ready = sem("gw_ready")
        gwT_made = sem("gwT_made")
        gwT_ready = sem("gwT_ready")
        tanh_ready = sem("tanh_ready")
        k_made = sem("k_made")
        kT_act = sem("kT_act")
        kT_dve = sem("kT_dve")
        wq_centred = sem("wq_centred")
        kq_made = sem("kq_made")
        kq_act = sem("kq_act")
        kq_dve = sem("kq_dve")
        cacc_ready = sem("cacc_ready")
        cbias_made = sem("cbias_made")
        cbias_ready = sem("cbias_ready")
        cg_made = sem("cg_made")
        cg_ready = sem("cg_ready")
        ctx_hi = sem("ctx_hi")
        ctx_lo = sem("ctx_lo")
        scale_hi = sem("scale_hi")
        scale_lo = sem("scale_lo")
        sign_ready = sem("sign_ready")
        gb_ready = sem("gb_ready")
        act_steps = sem("act_steps")
        dve_steps = sem("dve_steps")
        pool_steps = sem("pool_steps")
        scores_made = sem("scores_made")
        rstd0_ready = sem("rstd0_ready")
        nmax_ready = sem("nmax_ready")
        exp_ready = sem("exp_ready")
        e2_ready = sem("e2_ready")
        attT_made = sem("attT_made")
        att_hi_ready = sem("att_hi_ready")
        att_lo_ready = sem("att_lo_ready")
        attended_made = sem("attended_made")
        x1_ready = sem("x1_ready")
        x1b_ready = sem("x1b_ready")
        veps1_ready = sem("veps1_ready")
        rstd1_ready = sem("rstd1_ready")
        rbias_ready = sem("rbias_ready")
        rexp_ready = sem("rexp_ready")
        route_ready = sem("route_ready")
        routeT_made = sem("routeT_made")
        route_hi = sem("route_hi")
        route_lo = sem("route_lo")
        is_made = sem("is_made")
        os_made = sem("os_made")
        os_ready = sem("os_ready")
        a_ready = sem("a_ready")
        aT_made = sem("aT_made")
        aT_hi_ready = sem("aT_hi_ready")
        aT_lo_ready = sem("aT_lo_ready")
        ffn_made = sem("ffn_made")
        scaled_ready = sem("scaled_ready")
        y_ready = sem("y_ready")
        last_ffn_made = sem("last_ffn_made")
        last_y_ready = sem("last_y_ready")

        block = ctx.enter_context(nc.Block())

        def half(h):
            return slice(h * H, (h + 1) * H)

        def last_part(i):
            return slice(H + i * H // 2, H + (i + 1) * H // 2)

        def pairs(eng, steps, per_pair, iteration):
            with eng.Fori(0, (NT - 4) // 2) as i:
                if steps is not None:
                    start, steps.loop = steps.count, i * per_pair
                for c in range(2):
                    iteration(2 * i + (2 + c), c, (2 * i + (3 + c)) // TPB)
                if steps is not None:
                    assert steps.count - start == per_pair, steps.count - start
                    steps.loop, steps.count = 0, start + per_pair * ((NT - 4) // 2)

        @block.sync
        def _(sp):
            for c in range(CH):
                sp.dma_start(ctxT[:, c, :], ctx_cols[:, c, :]).then_inc(ctxT_loaded[c], 16)
                if c == 0:
                    sp.dma_start(wk3[:, c, half(0)], wk_cols[0:P, half(0)]).then_inc(wk0_loaded, 16)
                    sp.dma_start(wk3[:, c, half(1)], wk_cols[0:P, half(1)]).then_inc(wk_loaded[c], 16)
                else:
                    sp.dma_start(wk3[:, c, :], wk_cols[c * P:(c + 1) * P, :]).then_inc(wk_loaded[c], 16)
                if c == 1:
                    sp.dma_start(gw, gate_w).then_inc(gw_loaded, 16)
            for c in range(CH):
                sp.dma_start(wq3[:, c, :], wq_rows[c * P:(c + 1) * P, :]).then_inc(wq_loaded[c], 16)

            def load(t, s):
                sp.dma_start(xT_sb[:, s, :, :], x_cols[bass.ds(t * P, P), :, :]).then_inc(xT_loaded[s], 16)
                sp.dma_start(x_sb[:, s, :], x_rows[bass.ds(t * P, P), :]).then_inc(x_loaded[s], 16)

            for t in range(2):
                load(t, t)

            def load_w(c):
                sp.dma_start(w_raw[c], w_cols[c * P:(c + 1) * P, :]).then_inc(w_loaded[c], 16)

            for c in range(4):
                if c == 3:
                    sp.wait_ge(gwT_made, 1)
                load_w(c)
            for c in (4, 5):
                sp.wait_ge(sign_ready, c - 3)
                load_w(c)
            sp.wait_ge(k_made, CH)

            def load_context(b0):
                for d in range(2):
                    sp.dma_start(ctx_raw[d * NC:(d + 1) * NC, b0:b0 + 2, 0:D],
                                 ctx_rows[b0:b0 + 2].rearrange("b p d -> p b d")).then_inc(ctx_loaded[b0 // 2], 16)

            load_context(0)
            sp.wait_ge(scale_zero, 1)
            for g in range(4):
                for n, src in enumerate((in_scale, out_scale)):
                    sp.dma_start(scale_raw[g * GRP:g * GRP + E, n, :], src).then_inc(scale_loaded, 16)
            for c in (6, 7):
                sp.wait_ge(sign_ready, c - 1)
                load_w(c)
            load_context(2)
            sp.dma_start(bias_bc, ffn_bias.rearrange("(a n) -> a n", a=1).to_broadcast([P, D])).then_inc(bias_loaded, 16)

            def load_into_used(t, s):
                sp.wait_ge(scores_made, t - 1)
                sp.wait_ge(x1_ready, t - 1)
                load(t, s)

            def store(t, s):
                for h in range(2):
                    sp.wait_ge(y_ready, 2 * t + (h + 1))
                    sp.dma_start(y_rows[bass.ds(t * P, P), half(h)], y_sb[:, s, half(h)]).then_inc(y_free[s], 16)

            load_into_used(2, 0)
            sp.wait_ge(kq_later_made, CH)
            for s in range(2):
                sp.sem_inc(y_free[s], 16)
            load_into_used(3, 1)
            with sp.Fori(0, (NT - 4) // 2) as i:
                for c in range(2):
                    store(2 * i + c, c)
                    load_into_used(2 * i + (4 + c), c)
            for t in range(NT - 4, NT - 1):
                store(t, t % 2)
            sp.wait_ge(y_ready, 2 * NT - 1)
            sp.dma_start(y_rows[T - P:T, half(0)], y_sb[:, 1, half(0)]).then_inc(y_free[1], 16)
            for i in range(2):
                sp.wait_ge(last_y_ready, i + 1)
                sp.dma_start(y_rows[T - P:T, last_part(i)], y_sb[:, 1, last_part(i)]).then_inc(y_free[1], 16)
            sp.wait_ge(y_free[0], 32 * (NT // 2) + 16)
            sp.wait_ge(y_free[1], 32 * (NT // 2) + 32)

        @block.gpsimd
        def _(pool):
            steps = Steps(pool, pool_steps)
            steps.done(nc.gpsimd.memset(ident[:, :], 0.0))
            nc.gpsimd.memset(kqg4[:, :, :, NC + E:KW], 0.0)
            nc.gpsimd.memset(gwT[:, :, 0:NC], 0.0).then_inc(gwT_zero, 1)
            steps.wait()
            nc.gpsimd.affine_select(out=ident[:, :], in_=ident[:, :], compare_op=ALU.not_equal, fill=1.0, base=0,
                                    pattern=[[-1, P]], channel_multiplier=1).then_inc(consts, 1)
            nc.gpsimd.memset(eps_d[:, :], EPS * D)
            nc.gpsimd.memset(neg_half[:, :], -0.5)
            nc.gpsimd.memset(route[:, :, :], 0.0).then_inc(consts, 1)
            pool.wait_ge(k_made, CH)
            nc.gpsimd.memset(scale_raw, 0.0).then_inc(scale_zero, 1)

            def x_rstd(t):
                pool.wait_ge(ssq0_ready, t + 1)
                steps.done(nc.gpsimd.tensor_tensor(veps0[:, :], ssq0[:, :], eps_d[:, :], ALU.add))
                steps.wait()
                nc.gpsimd.tensor_tensor(rstd0[:, :], veps0[:, :], neg_half[:, :], ALU.pow).then_inc(rstd0_ready, 1)

            def iteration(j, s, b=None, prev=True, cur=True, nxt=True):
                def add_up(h):
                    if h == 0:
                        pool.wait_ge(x1b_ready, j)
                    pool.wait_ge(scaled_ready, 2 * j + (h - 1))
                    nc.gpsimd.tensor_tensor(y_sb[:, 1 - s, half(h)], y_sb[:, 1 - s, half(h)],
                                            x1b[:, 1 - s, half(h)], ALU.add).then_inc(y_ready, 1)

                if prev:
                    add_up(0)
                    if cur:
                        add_up(1)
                if cur:
                    if prev:
                        pool.wait_ge(y_ready, 2 * j)
                    nc.gpsimd.tensor_tensor(x1b[:, s, :], x1[:, s, :], bias_bc, ALU.add).then_inc(x1b_ready, 1)
                if nxt and not (isinstance(j, int) and j + 2 >= NT):
                    x_rstd(j + 2)
                if nxt:
                    pool.wait_ge(veps1_ready, j + 2)
                    nc.gpsimd.tensor_tensor(rstd1[:, 1 - s:2 - s], veps1[:, :], neg_half[:, :], ALU.pow)\
                      .then_inc(rstd1_ready, 1)

            pool.wait_ge(consts, 2)
            x_rstd(0)
            pool.wait_ge(rstd0_ready, 1)
            pool.wait_ge(scale_hi, 1)
            for g in (1, 3):
                if g == 3:
                    pool.wait_ge(scale_lo, 1)
                rows = slice(g * GRP, (g + 1) * GRP)
                nc.gpsimd.tensor_tensor(scales[rows, :, :], scale_raw[rows, :, :], scales[rows, :, :].bitcast(f32),
                                        ALU.subtract).then_inc(scale_lo, 1)
            pool.wait_ge(scale_lo, 2)
            pool.wait_ge(gb_ready, 1)
            iteration(-1, 1, prev=False, cur=False)
            iteration(0, 0, prev=False)
            iteration(1, 1)
            pairs(pool, steps, 2, iteration)
            iteration(NT - 2, 0)
            iteration(NT - 1, 1, nxt=False)
            iteration(NT, 0, cur=False, nxt=False)

        @block.scalar
        def _(act):
            act.dma_start(bqT[:, :], bq_cols).then_inc(small_loaded, 16)
            act.dma_start(bkT[:, :], bk_cols).then_inc(small_loaded, 16)
            act.dma_start(gates[:, 0:1], g_xattn.rearrange("(a n) -> a n", a=1).to_broadcast([P, 1])).then_inc(small_loaded, 16)
            act.dma_start(gates[:, 1:2], g_ffn.rearrange("(a n) -> a n", a=1).to_broadcast([P, 1])).then_inc(small_loaded, 16)
            steps = Steps(act, act_steps)
            for c in range(CH):
                act.wait_ge(wq_loaded[c], 16)
                nc.scalar.activation(signT[:, c, :], wq3[:, c, :], ACT.Copy, scale=1.0 / D,
                                     accum_out=wq_mean[:, c:c + 1]).then_inc(wq_means, 1)
            act.wait_ge(small_loaded, 64)
            nc.scalar.activation(tgates[:, :], gates[:, :], ACT.Tanh).then_inc(tanh_ready, 1)

            def x_statistics(t, s, out):
                act.wait_ge(x_loaded[s], 16 * (t // 2) + 16)
                steps.done(nc.scalar.activation(out, x_sb[:, s, :], ACT.Copy, scale=-1.0 / D,
                                                accum_out=nmean0[:, 0:1]))
                steps.wait()
                nc.scalar.activation(out, x_sb[:, s, :], ACT.Square, bias=nmean0[:, 0:1],
                                     accum_out=ssq0[:, 0:1]).then_inc(ssq0_ready, 1)

            for c in range(0, CH, 2):
                act.wait_ge(k_made, c + 1)
                nc.scalar.activation(kT[:, c, :], bank[c][:, 0:CTX], ACT.Identity, bias=bkT[:, c:c + 1]).then_inc(kT_act, 1)
            act.wait_ge(wq_means, CH)
            x_statistics(0, 0, signT[:, 0, :])

            def context_high(b):
                act.wait_ge(ctx_loaded[b // 2], 32)
                nc.scalar.activation(ctxs3[:, b, :], ctx_raw[:, b, :], ACT.Copy).then_inc(ctx_hi, 1)

            def signs(chunks):
                for n in chunks:
                    act.wait_ge(w_loaded[n], 16)
                    nc.scalar.activation(signT[:, n, :], w_raw[n], ACT.Sign).then_inc(sign_ready, 1)

            def kq_out(m, first, made, ready):
                act.wait_ge(made, m + 1)
                src = bank[m if first == 0 else LATER[m]][:, 0:2 * NC].rearrange("p (b n) -> p b n", b=2)
                nc.scalar.activation(kqg4[:, first:first + 2, m, 0:NC], src, ACT.Copy).then_inc(ready, 1)

            act.wait_ge(ssq0_ready, 1)
            signs(range(0, 2))
            kq_out(0, 0, kq_made, kq_act)
            for m in range(CTX // P):
                act.wait_ge(cg_made, m + 1)
                nc.scalar.activation(cgs[:, m, :], bank[5 + m][:, NC:NC + E], ACT.Copy).then_inc(cg_ready, 1)
            signs(range(2, 4))
            kq_out(2, 0, kq_made, kq_act)
            signs(range(4, 6))
            kq_out(4, 0, kq_made, kq_act)
            act.wait_ge(cbias_made, 1)
            nc.scalar.activation(cbias[:, :], bank[7][:, 0:CTX], ACT.Copy, scale=SC).then_inc(cbias_ready, 1)
            act.wait_ge(scale_loaded, 16 * 8)
            nc.scalar.activation(scales[:, :, :], scale_raw, ACT.Copy).then_inc(scale_hi, 1)
            kq_out(6, 0, kq_made, kq_act)
            act.wait_ge(gates_copied, 1)
            context_high(0)
            context_high(1)
            kq_out(0, 2, kq_later_made, kq_later_ready)
            context_high(2)

            def iteration(j, s, b=None, prev=True, cur=True, nxt=True, later=0):
                if cur:
                    act.wait_ge(routeT_made, j + 1)
                    nc.scalar.activation(routeT[:, :], bank[2][:, 0:P], ACT.Copy).then_inc(route_hi, 1)
                if nxt:
                    act.wait_ge(nmax_ready, j + 2)
                    nc.scalar.activation(e_sb[:, :], s_sb[:, :], ACT.Exp, bias=nmax[:, 0:1],
                                         accum_out=esum[:, 0:1]).then_inc(exp_ready, 1)
                if later == 2:
                    kq_out(5, 2, kq_later_made, kq_later_ready)
                if cur:
                    for h in range(2):
                        act.wait_ge(os_made, 2 * j + (h + 1))
                        nc.scalar.activation(os_sb[:, s, half(h)], bank[h][:, :], ACT.Copy).then_inc(os_ready, 1)
                if later == 1:
                    context_high(3)
                    kq_out(1, 2, kq_later_made, kq_later_ready)
                if nxt:
                    act.wait_ge(attT_made, j + 2)
                    nc.scalar.activation(att_hi[:, :], bank[7][:, 0:P], ACT.Copy).then_inc(att_hi_ready, 1)
                if later == 1:
                    x_statistics(1, 1, junk)
                    kq_out(2, 2, kq_later_made, kq_later_ready)
                    signs(range(6, CH))
                if later == 2:
                    kq_out(6, 2, kq_later_made, kq_later_ready)
                if cur:
                    for h in range(2):
                        act.wait_ge(aT_made, 2 * j + (h + 1))
                        nc.scalar.activation(aT_hi[:, s, h * CH // 2:(h + 1) * CH // 2, :],
                                             bank[3 + h][:, :].rearrange("p (c t) -> p c t", t=P), ACT.Copy)\
                          .then_inc(aT_hi_ready, 1)
                if later == 1:
                    for m in range(3, 5):
                        kq_out(m, 2, kq_later_made, kq_later_ready)
                if later == 2:
                    kq_out(7, 2, kq_later_made, kq_later_ready)
                if nxt and not (isinstance(j, int) and not 0 <= j < NT - 2):
                    x_statistics(j + 2, s, junk)
                if nxt:
                    act.wait_ge(rbias_ready, j + 2)
                    nc.scalar.activation(eroute[:, :], logit[:, :], ACT.Exp, bias=rbias[:, 0:1],
                                         scale=rstd1[:, 1 - s:2 - s], accum_out=rsum[:, 0:1]).then_inc(rexp_ready, 1)

            iteration(-1, 1, prev=False, cur=False, later=1)
            iteration(0, 0, prev=False, later=2)
            iteration(1, 1)
            pairs(act, steps, 2, iteration)
            iteration(NT - 2, 0)
            iteration(NT - 1, 1, nxt=False)

        @block.vector
        def _(dve):
            steps = Steps(dve, dve_steps)

            def mean_var(src, out):
                for h in range(2):
                    last = nc.vector.bn_stats(st[0:src.shape[0], h, :], src[:, half(h)])
                steps.done(last)
                steps.wait()
                nc.vector.memset(hold[:, :], 0.0)
                steps.done(nc.vector.bn_aggr(out, st[0:src.shape[0], :, :]))
                steps.wait()

            nc.vector.memset(ones[:, :], 1.0).then_inc(ones_ready, 1)
            dve.wait_ge(gw_loaded, 16)
            mean_var(gw, mv0[0:E, :])
            nc.vector.tensor_scalar(gw, gw, mv0[0:E, 0:1], None, ALU.subtract).then_inc(gw_ready, 1)
            for c in range(CH):
                dve.wait_ge(wq_means, c + 1)
                nc.vector.tensor_scalar(wq3[:, c, :], wq3[:, c, :], wq_mean[:, c:c + 1], None, ALU.subtract).then_inc(wq_centred, 1)
            dve.wait_ge(small_loaded, 64)
            for c in range(1, CH, 2):
                dve.wait_ge(k_made, c + 1)
                nc.vector.tensor_scalar(kT[:, c, :], bank[c][:, 0:CTX], bkT[:, c:c + 1], None, ALU.add).then_inc(kT_dve, 1)
            dve.wait_ge(gwT_zero, 1)
            dve.wait_ge(gwT_made, 1)
            turned = bank[2][:, 0:CH * E].rearrange("p (c e) -> p c e", e=E)
            for b in range(NB):
                last = nc.vector.tensor_copy(kqg4[:, b, :, NC:NC + E], turned)
            last.then_inc(gwT_ready, 1)
            dve.wait_ge(kT_dve, CH // 2)
            dve.wait_ge(kT_act, CH // 2)
            for c in range(CH):
                if c == 0:
                    ins = nc.vector.tensor_scalar(cacc[:, :], kT[:, c, :], bqT[:, c:c + 1], None, ALU.mult)
                else:
                    ins = nc.vector.scalar_tensor_tensor(out=cacc[:, :], in0=kT[:, c, :], scalar=bqT[:, c:c + 1],
                                                         in1=cacc[:, :], op0=ALU.mult, op1=ALU.add)
                if c == CH - 1:
                    ins.then_inc(cacc_ready, 1)
                else:
                    steps.done(ins)
                    steps.wait()

            dve.wait_ge(cg_ready, CTX // P)
            for b in range(NB):
                rows = slice((b % 2) * NC, (b % 2 + 1) * NC)
                for d in range(2):
                    last = nc.vector.tensor_copy(ctx_raw[d * NC:(d + 1) * NC, b, D:CW], cgs[rows, b // 2, :])
            last.then_inc(gates_copied, 1)

            def context_low(b):
                dve.wait_ge(ctx_hi, b + 1)
                nc.vector.tensor_tensor(ctxs3[NC:P, b, :], ctx_raw[NC:P, b, :], ctxs3[NC:P, b, :].bitcast(f32),
                                        ALU.subtract).then_inc(ctx_lo, 1)

            def kq_out(m):
                dve.wait_ge(kq_made, m + 1)
                nc.vector.tensor_copy(kqg4[:, 0:2, m, 0:NC], bank[m][:, 0:2 * NC].rearrange("p (b n) -> p b n", b=2))\
                  .then_inc(kq_dve, 1)

            for m in range(1, CH, 2):
                kq_out(m)
            for b in range(2):
                context_low(b)

            def iteration(j, s, b=None, prev=True, cur=True, nxt=True, first=False):
                n = 1 - s

                def scale_output(h):
                    dve.wait_ge(ffn_made, 2 * j + (h - 1))
                    nc.vector.scalar_tensor_tensor(out=y_sb[:, n, half(h)], in0=bank[5 + h][:, :],
                                                   scalar=rfin[:, n:n + 1], in1=os_sb[:, n, half(h)],
                                                   op0=ALU.mult, op1=ALU.mult).then_inc(scaled_ready, 1)

                def low_half(h):
                    dve.wait_ge(aT_hi_ready, 2 * j + (h + 1))
                    chunks = slice(h * CH // 2, (h + 1) * CH // 2)
                    nc.vector.tensor_tensor(aT_lo[:, s, chunks, :], bank[3 + h][:, :].rearrange("p (c t) -> p c t", t=P),
                                            aT_hi[:, s, chunks, :].bitcast(f32), ALU.subtract).then_inc(aT_lo_ready, 1)

                if nxt:
                    dve.wait_ge(scores_made, j + 2)
                    dve.wait_ge(rstd0_ready, j + 2)
                    steps.done(nc.vector.scalar_tensor_tensor(
                        out=s_sb[:, :], in0=bank[7][:, 0:NC], scalar=rstd0[:, 0:1],
                        in1=cbias[:, bass.ds(b * NC, NC)], op0=ALU.mult, op1=ALU.add))
                    nc.vector.tensor_copy(xgate[:, n, :], bank[7][:, NC:NC + E])
                    steps.wait()
                    nc.vector.reduce_max(nmax[:, :], s_sb[:, :], AX.X, negate=True).then_inc(nmax_ready, 1)
                if cur:
                    dve.wait_ge(route_hi, j + 1)
                    nc.vector.tensor_tensor(routeT[NC:P, :], bank[2][NC:P, 0:P], routeT[NC:P, :].bitcast(f32),
                                            ALU.subtract).then_inc(route_lo, 1)
                if prev:
                    dve.wait_ge(y_free[n], 32 * ((j - 1) // 2) + 16)
                    scale_output(0)
                if nxt:
                    dve.wait_ge(exp_ready, j + 2)
                    steps.done(nc.vector.reciprocal(erec[:, :], esum[:, :]))
                    steps.wait()
                    nc.vector.tensor_scalar(e2[:, :, :], e_sb[:, :].unsqueeze(1).to_broadcast([P, 2, NC]),
                                            erec[:, 0:1], tgates[:, 0:1], ALU.mult, ALU.mult).then_inc(e2_ready, 1)
                if first:
                    context_low(2)
                if cur:
                    for h in range(2):
                        dve.wait_ge(is_made, 2 * j + (h + 1))
                        nc.vector.scalar_tensor_tensor(out=a_sb[:, half(h)], in0=x1[:, s, half(h)],
                                                       scalar=mv1[:, s, 0:1], in1=bank[3 + h][:, :],
                                                       op0=ALU.subtract, op1=ALU.mult).then_inc(a_ready, 1)
                if nxt:
                    dve.wait_ge(att_hi_ready, j + 2)
                    nc.vector.tensor_tensor(att_lo[:, :], bank[7][:, 0:P], att_hi[:, :].bitcast(f32),
                                            ALU.subtract).then_inc(att_lo_ready, 1)
                if prev and cur:
                    scale_output(1)
                if prev and not cur:
                    dve.wait_ge(x1b_ready, j)
                    for i in range(2):
                        part = last_part(i)
                        dve.wait_ge(last_ffn_made, i + 1)
                        steps.done(nc.vector.scalar_tensor_tensor(
                            out=y_sb[:, n, part], in0=bank[(6, 0)[i]][:, 0:H // 2], scalar=rfin[:, n:n + 1],
                            in1=os_sb[:, n, part], op0=ALU.mult, op1=ALU.mult))
                        steps.wait()
                        nc.vector.tensor_tensor(y_sb[:, n, part], y_sb[:, n, part], x1b[:, n, part], ALU.add)\
                          .then_inc(last_y_ready, 1)
                if first:
                    context_low(3)
                    dve.wait_ge(bias_loaded, 16)
                    nc.vector.tensor_scalar(bias_bc, bias_bc, tgates[:, 1:2], None, ALU.mult).then_inc(gb_ready, 1)
                if cur:
                    low_half(0)
                    low_half(1)
                if nxt:
                    dve.wait_ge(attended_made, j + 2)
                    if not (isinstance(j, int) and j < 1):
                        dve.wait_ge(x1b_ready, j)
                    for i in range(3):
                        cols = slice(i * AW, min((i + 1) * AW, D))
                        last = nc.vector.tensor_tensor(x1[:, n, cols], x_sb[:, n, cols],
                                                       bank[i][:, 0:cols.stop - cols.start], ALU.add)
                    last.then_inc(x1_ready, 1)
                    steps.done(nc.vector.tensor_tensor(logit[:, :], xgate[:, n, :], bank[2][:, D - 2 * AW:AW], ALU.add))
                    dve.wait_ge(x1_ready, j + 2)
                    mean_var(x1[:, n, :], mv1[:, n, :])
                    nc.vector.tensor_scalar(veps1[:, :], mv1[:, n, 1:2], EPS, None, ALU.add).then_inc(veps1_ready, 1)
                    steps.wait()
                    steps.done(nc.vector.reduce_max(rmax[:, :], logit[:, :], AX.X, negate=True))
                    steps.wait()
                    dve.wait_ge(rstd1_ready, j + 2)
                    nc.vector.tensor_scalar(rbias[:, :], rmax[:, :], rstd1[:, n:n + 1], None, ALU.mult)\
                      .then_inc(rbias_ready, 1)
                    nc.vector.tensor_scalar(rfin[:, n:n + 1], rstd1[:, n:n + 1], tgates[:, 1:2], None, ALU.mult)
                    dve.wait_ge(rexp_ready, j + 2)
                    steps.done(nc.vector.reciprocal(rrec[:, :], rsum[:, :]))
                    steps.wait()
                    nc.vector.tensor_scalar(route[:, :, 0:E], eroute[:, :].unsqueeze(1).to_broadcast([P, 4, E]),
                                            rrec[:, 0:1], None, ALU.mult).then_inc(route_ready, 1)

            dve.wait_ge(cbias_ready, 1)
            dve.wait_ge(tanh_ready, 1)
            iteration(-1, 1, 0, prev=False, cur=False, first=True)
            iteration(0, 0, 0, prev=False)
            iteration(1, 1, 0)
            pairs(dve, steps, 2 * 7, iteration)
            iteration(NT - 2, 0, NB - 1)
            iteration(NT - 1, 1, nxt=False)
            iteration(NT, 0, cur=False, nxt=False)

        @block.tensor
        def _(pe):
            pe.wait_ge(ones_ready, 1)
            for _ in range(WARM):
                nc.tensor.matmul(bank[7][:, 0:P], ones[:, :], ones[:, :], start=True, stop=True)
            for c in range(CH):
                pe.wait_ge(ctxT_loaded[c], 16)
                pe.wait_ge(wk0_loaded if c == 0 else wk_loaded[c], 16)
                for m in range(CH):
                    if c == 0 and m == CH // 2:
                        pe.wait_ge(wk_loaded[0], 16)
                    last = nc.tensor.matmul(bank[m][:, 0:CTX], wk3[:, c, m * P:(m + 1) * P], ctxT[:, c, :],
                                            start=(c == 0), stop=(c == CH - 1))
                    if c == CH - 1:
                        last.then_inc(k_made, 1)
            pe.wait_ge(consts, 1)
            pe.wait_ge(gw_ready, 1)
            pe.wait_ge(kT_act, 2)
            for c in range(CH):
                last = nc.tensor.transpose(bank[2][:, c * E:(c + 1) * E], gw[:, c * P:(c + 1) * P],
                                           ident[0:E, 0:E])
            last.then_inc(gwT_made, 1)

            def kq(out, m, first, made):
                for c in range(CH):
                    last = nc.tensor.matmul(out[:, 0:2 * NC], wq3[:, c, m * P:(m + 1) * P],
                                            kT[:, c, first * NC:(first + 2) * NC], start=(c == 0), stop=(c == CH - 1))
                last.then_inc(made, 1)

            pe.wait_ge(wq_centred, CH)
            pe.wait_ge(kT_act, CH // 2)
            pe.wait_ge(kT_dve, CH // 2)
            for m in range(CH):
                if m == 2:
                    pe.wait_ge(gwT_ready, 1)
                    for i in range(CTX // P):
                        for c in range(CH):
                            last = nc.tensor.matmul(bank[5 + i][:, 0:KW], ctxT[:, c, i * P:(i + 1) * P], gwT[:, c, :],
                                                    start=(c == 0), stop=(c == CH - 1))
                        last.then_inc(cg_made, 1)
                if m in (5, 6):
                    pe.wait_ge(cg_ready, m - 4)
                if m == 4:
                    pe.wait_ge(cacc_ready, 1)
                    nc.tensor.matmul(bank[7][:, 0:CTX], ones[:, :], cacc[:, :], start=True, stop=True)\
                      .then_inc(cbias_made, 1)
                if m == 7:
                    pe.wait_ge(cbias_ready, 1)
                kq(bank[m], m, 0, kq_made)

            def kq_later(m):
                if LATER[m] in LATER[:m]:
                    before = max(k for k in range(m) if LATER[k] == LATER[m])
                    pe.wait_ge(kq_later_ready, before + 1)
                kq(bank[LATER[m]], m, 2, kq_later_made)

            def ffn(t, s, quarters):
                for q in quarters:
                    h, part = q // 4, q % 4 // 2
                    if q % 4 == 0 and not (isinstance(t, int) and t < 1):
                        pe.wait_ge(scaled_ready, 2 * t + (h - 1))
                    if q < 2:
                        pe.wait_ge(aT_hi_ready, 2 * t + (q + 1))
                    if q == 2:
                        pe.wait_ge(aT_lo_ready, 2 * t + 2)
                    src = (aT_hi, aT_lo)[part]
                    for c in range(q % 2 * 4, q % 2 * 4 + 4):
                        last = nc.tensor.matmul(bank[5 + h][:, :], src[:, s, c, :], signT[:, c, half(h)],
                                                start=(part == 0 and c == 0), stop=(part == 1 and c == CH - 1))
                    if q % 4 == 3:
                        last.then_inc(ffn_made, 1)

            def iteration(j, s, b=None, prev=True, cur=True, nxt=True, later=0):
                n = 1 - s
                if prev:
                    ffn(j - 1, n, range(4))
                if nxt:
                    pe.wait_ge(xT_loaded[n], 16 * ((j + 1) // 2) + 16)
                    for c in range(CH):
                        last = nc.tensor.matmul(bank[7][:, 0:KW], xT_sb[:, n, c, :],
                                                kqg[:, bass.ds(b * (CH * KW) + c * KW, KW)],
                                                start=(c == 0), stop=(c == CH - 1))
                    last.then_inc(scores_made, 1)
                if prev:
                    ffn(j - 1, n, range(4, 5 if nxt else 6))
                if cur:
                    pe.wait_ge(route_ready, j + 1)
                    nc.tensor.transpose(bank[2][:, 0:P], route[:, :, :].rearrange("p g e -> p (g e)"), ident[:, :])\
                      .then_inc(routeT_made, 1)
                if prev:
                    ffn(j - 1, n, range(5 if nxt else 6, 7))
                if later == 2:
                    kq_later(5)
                    pe.wait_ge(scale_lo, 2)
                    pe.wait_ge(kq_later_ready, 5)
                if cur:
                    pe.wait_ge(route_hi, j + 1)
                    pe.wait_ge(route_lo, j + 1)
                    for k, first, made in ((0, 3, is_made), (1, 0, os_made)):
                        for h in range(2):
                            nc.tensor.matmul(bank[first + h][:, :], routeT[:, :], scales[:, k, half(h)],
                                             start=True, stop=True).then_inc(made, 1)
                if later == 1:
                    kq_later(1)
                if nxt:
                    pe.wait_ge(e2_ready, j + 2)
                    nc.tensor.transpose(bank[7][:, 0:P], e2[:, :, :].rearrange("p a n -> p (a n)"), ident[:, :])\
                      .then_inc(attT_made, 1)
                if later == 1:
                    kq_later(2)
                if later == 2:
                    kq_later(6)
                if prev:
                    ffn(j - 1, n, range(7, 8))
                if cur:
                    for h in range(2):
                        pe.wait_ge(a_ready, 2 * j + (h + 1))
                        for c in range(CH // 2):
                            k = h * CH // 2 + c
                            last = nc.tensor.transpose(bank[3 + h][:, c * P:(c + 1) * P], a_sb[:, k * P:(k + 1) * P],
                                                       ident[:, :])
                        last.then_inc(aT_made, 1)
                if later == 2:
                    kq_later(7)
                if nxt:
                    if later == 1:
                        pe.wait_ge(ctx_lo, 1)
                    pe.wait_ge(att_hi_ready, j + 2)
                    pe.wait_ge(att_lo_ready, j + 2)
                    if not (isinstance(j, int) and j < 0):
                        pe.wait_ge(os_ready, 2 * j + 2)
                    for i in range(3):
                        for part, src in enumerate((att_hi, att_lo)):
                            last = nc.tensor.matmul(bank[i][:, 0:AW], src[:, :], ctxs[:, bass.ds(b * CW + i * AW, AW)],
                                                    start=(part == 0), stop=(part == 1))
                    last.then_inc(attended_made, 1)
                if later == 1:
                    for m in range(3, 5):
                        kq_later(m)

            pe.wait_ge(kq_dve, 2)
            kq_later(0)
            pe.wait_ge(kq_act, CH // 2)
            pe.wait_ge(kq_dve, CH // 2)
            iteration(-1, 1, 0, prev=False, cur=False, later=1)
            iteration(0, 0, 0, prev=False, later=2)
            pe.wait_ge(kq_later_ready, CH)
            pe.wait_ge(sign_ready, CH)
            iteration(1, 1, 0)
            pe.wait_ge(ctx_lo, NB)
            pairs(pe, None, 0, iteration)
            iteration(NT - 2, 0, NB - 1)
            iteration(NT - 1, 1, nxt=False)
            ffn(NT - 1, 1, range(4))
            for i in range(2):
                if i == 0:
                    pe.wait_ge(scaled_ready, 2 * NT - 2)
                for part, src in enumerate((aT_hi, aT_lo)):
                    for c in range(CH):
                        last = nc.tensor.matmul(bank[(6, 0)[i]][:, 0:H // 2], src[:, 1, c, :], signT[:, c, last_part(i)],
                                                start=(part == 0 and c == 0), stop=(part == 1 and c == CH - 1))
                last.then_inc(last_ffn_made, 1)


def kernel(**inputs):
    import numpy as np
    import concourse.bacc as bacc
    from concourse.bass_utils import run_bass_kernel_spmd

    P = 128
    a = {k: np.asarray(v) for k, v in inputs.items()}
    x = a["x"].reshape(-1, a["x"].shape[-1])
    T, D = x.shape
    CH = D // P
    ctx = a["ctx_4096"]

    def columns(v):
        return v.reshape(CH, P, -1).transpose(1, 0, 2)

    arrays = {
        "x_rows": x,
        "x_cols": x.reshape(T // P, P, CH, P).transpose(0, 3, 2, 1).reshape(T, CH, P),
        "ctx_rows": ctx,
        "ctx_cols": columns(ctx.reshape(-1, D).T),
        "g_xattn": a["g_xattn"],
        "g_ffn": a["g_ffn"],
        "wq_rows": a["L0_xattn_Wq"],
        "bq_cols": columns(a["L0_xattn_bq"][:, None])[:, :, 0],
        "wk_cols": a["L0_xattn_Wk"].T,
        "bk_cols": columns(a["L0_xattn_bk"][:, None])[:, :, 0],
        "w_cols": a["L0_ffn_weight"].T,
        "ffn_bias": a["L0_ffn_bias"],
        "gate_w": a["L0_ffn_gate_w"],
        "in_scale": a["L0_ffn_in_channel_scale"],
        "out_scale": a["L0_ffn_out_channel_scale"],
    }
    nc = bacc.Bacc("TRN2", target_bir_lowering=False, num_devices=1)
    feeds, args = {}, []
    for name, v in arrays.items():
        v = np.ascontiguousarray(v)
        feeds[f"in_{name}"] = v
        args.append(nc.dram_tensor(f"in_{name}", v.shape, mybir.dt.from_np(v.dtype), kind="ExternalInput").ap())
    args.append(nc.dram_tensor("out_y", (T, D), mybir.dt.float32, kind="ExternalOutput").ap())
    gated_cross_attention_and_routed_ffn(nc, *args)
    r = run_bass_kernel_spmd(nc, [feeds], core_ids=[0])
    return r.results[0]["out_y"].reshape(a["x"].shape)
```
